# Optimizing a Trainium2 kernel written in Bass

```python
import numpy as np
import jax
import jax.numpy as jnp

def _softmax(x, axis=-1):
    return jax.nn.softmax(x, axis=axis)

def _gelu(x):
    return jax.nn.gelu(x, approximate=True)

def _silu(x):
    return jax.nn.silu(x)

def _sigmoid(x):
    return jax.nn.sigmoid(x)

def _layernorm(x, axis=-1, eps=1e-05):
    m = jnp.mean(x, axis=axis, keepdims=True)
    v = jnp.var(x, axis=axis, keepdims=True)
    return (x - m) / jnp.sqrt(v + eps)

def _scatter_add(tgt, idx, src, axis=0):
    return tgt.at[idx].add(src)

def _segment_sum(src, seg, n):
    return jax.ops.segment_sum(src, seg, n)
kernel_name = 'mk_xattn_ffn_d1_seqx_r8_db868c'

def setup_inputs(seed: int=0):
    np.random.seed(seed)
    _w = jnp.asarray

    def _rec_inputs():
        import jax
        import jax.numpy as jnp
        _rk = jax.random.key(seed)
        x = 7.22e-05 + 1 * jax.random.normal(jax.random.fold_in(_rk, 1), (16, 128, 256), jnp.float32)
        _lenS = 128 - jax.random.randint(jax.random.fold_in(_rk, 7), (16,), 0, max(1, 128 // 4) + 1, jnp.int32)
        _lenS2 = 128 - jax.random.randint(jax.random.fold_in(_rk, 8), (16,), 0, max(1, 128 // 4) + 1, jnp.int32)
        _ctx_512P = jax.random.normal(jax.random.fold_in(_rk, 11), (16, 16, 64), jnp.float32)
        _ctx_512c = jax.random.dirichlet(jax.random.fold_in(_rk, 511), 0.3 * jnp.ones((16,), jnp.float32), (16, 128))
        _ctx_512t = jnp.einsum('bsk,bkd->bsd', _ctx_512c, _ctx_512P)
        _ctx_512t = _ctx_512t * jax.lax.rsqrt(jnp.mean(jnp.square(_ctx_512t)) + 1e-12) * 0.953939
        ctx_512 = -0.000514642 + 1.00011 * (_ctx_512t + 0.3 * jax.random.normal(jax.random.fold_in(_rk, 611), (16, 128, 64), jnp.float32))
        return (x, ctx_512)
    x, ctx_512 = _rec_inputs()

    def _L0_xattn_setup():
        import jax, jax.numpy as jnp
        import numpy as np
        import math
        D_MODEL = 256
        N_HEADS = 16
        N_GROUPS = 4
        HEADS_PER_GROUP = N_HEADS // N_GROUPS
        HEAD_DIM = D_MODEL // N_HEADS
        B, S = (2, 256)
        key = jax.random.key(seed)
        k1, k2, k3, k4, k5 = jax.random.split(key, 5)
        q = jax.random.normal(k1, (B, S, D_MODEL), dtype=jnp.float32)
        k = jax.random.normal(k2, (B, S, N_GROUPS * HEAD_DIM), dtype=jnp.float32)
        v = jax.random.normal(k3, (B, S, N_GROUPS * HEAD_DIM), dtype=jnp.float32)
        lim = 1.0 / math.sqrt(D_MODEL)
        Wc = jax.random.uniform(k4, (D_MODEL, D_MODEL), minval=-lim, maxval=lim, dtype=jnp.float32)
        bc = jax.random.uniform(k5, (D_MODEL,), minval=-lim, maxval=lim, dtype=jnp.float32)
        return {'q': q, 'k': k, 'v': v, 'Wc': Wc, 'bc': bc}
    _L0_xattn_all = _L0_xattn_setup()
    _L0_xattn_in = {k: v for k, v in _L0_xattn_all.items() if k in ('Wc', 'bc')}
    del _L0_xattn_all

    def _L0_ffn_setup():
        import jax, jax.numpy as jnp
        import numpy as np
        H = 256
        I = 128
        K = 8
        E = 128
        TOPK = 4
        EPS = 1e-08
        key = jax.random.key(seed)
        ks = jax.random.split(key, 10)
        s = 0.02
        return {'x': jax.random.normal(ks[0], (4, 256, H), jnp.float32), 'w_router': jax.random.normal(ks[1], (H, E), jnp.float32) * s, 'w_gate': jax.random.normal(ks[2], (H, K * I), jnp.float32) * s, 'w_up': jax.random.normal(ks[3], (H, K * I), jnp.float32) * s, 'w_down': jax.random.normal(ks[4], (I, H), jnp.float32) * s, 'amplitudes': jax.random.normal(ks[5], (E, K, 2), jnp.float32) * 0.1, 'expert_scale': jnp.ones((E,), jnp.float32), 'shared_w_gate': jax.random.normal(ks[6], (H, 2 * I), jnp.float32) * s, 'shared_w_up': jax.random.normal(ks[7], (H, 2 * I), jnp.float32) * s, 'shared_w_down': jax.random.normal(ks[8], (2 * I, H), jnp.float32) * s}
    _L0_ffn_all = _L0_ffn_setup()
    _L0_ffn_in = {k: v for k, v in _L0_ffn_all.items() if k in ('w_router', 'w_gate', 'w_up', 'w_down', 'amplitudes', 'expert_scale', 'shared_w_gate', 'shared_w_up', 'shared_w_down')}
    del _L0_ffn_all
    return {'x': x, 'ctx_512': ctx_512, 'L0_xattn_Wc': _L0_xattn_in['Wc'], 'L0_xattn_bc': _L0_xattn_in['bc'], 'L0_ffn_w_router': _L0_ffn_in['w_router'], 'L0_ffn_w_gate': _L0_ffn_in['w_gate'], 'L0_ffn_w_up': _L0_ffn_in['w_up'], 'L0_ffn_w_down': _L0_ffn_in['w_down'], 'L0_ffn_amplitudes': _L0_ffn_in['amplitudes'], 'L0_ffn_expert_scale': _L0_ffn_in['expert_scale'], 'L0_ffn_shared_w_gate': _L0_ffn_in['shared_w_gate'], 'L0_ffn_shared_w_up': _L0_ffn_in['shared_w_up'], 'L0_ffn_shared_w_down': _L0_ffn_in['shared_w_down']}

def reference(x, ctx_512, L0_xattn_Wc, L0_xattn_bc, L0_ffn_w_router, L0_ffn_w_gate, L0_ffn_w_up, L0_ffn_w_down, L0_ffn_amplitudes, L0_ffn_expert_scale, L0_ffn_shared_w_gate, L0_ffn_shared_w_up, L0_ffn_shared_w_down):
    import jax
    import jax.numpy as jnp

    def _L0_xattn_ref(q, k, v, Wc, bc):
        import jax, jax.numpy as jnp
        import numpy as np
        import math
        D_MODEL = 256
        N_HEADS = 16
        N_GROUPS = 4
        HEADS_PER_GROUP = N_HEADS // N_GROUPS
        HEAD_DIM = D_MODEL // N_HEADS
        B, S = (2, 256)
        b, s, _ = q.shape
        qh = q.reshape(b, s, N_GROUPS, HEADS_PER_GROUP, HEAD_DIM).transpose(0, 2, 3, 1, 4)
        kh = k.reshape(b, s, N_GROUPS, HEAD_DIM).transpose(0, 2, 1, 3)
        vh = v.reshape(b, s, N_GROUPS, HEAD_DIM).transpose(0, 2, 1, 3)
        scale = 1.0 / math.sqrt(HEAD_DIM)
        scores = jnp.einsum('bghsd,bgtd->bghst', qh, kh) * scale
        probs = jax.nn.softmax(scores, axis=-1)
        out = jnp.einsum('bghst,bgtd->bghsd', probs, vh)
        out = out.transpose(0, 3, 1, 2, 4).reshape(b, s, D_MODEL)
        return out @ Wc.T + bc

    def _L0_ffn_ref(x, w_router, w_gate, w_up, w_down, amplitudes, expert_scale, shared_w_gate, shared_w_up, shared_w_down):
        import jax, jax.numpy as jnp
        import numpy as np
        H = 256
        I = 128
        K = 8
        E = 128
        TOPK = 4
        EPS = 1e-08
        B, S, _ = x.shape
        T = B * S
        xt = x.reshape(T, H)
        probs = jax.nn.softmax(xt @ w_router, axis=-1)
        topk_p, topk_idx = jax.lax.top_k(probs, TOPK)
        topk_w = topk_p / (jnp.sum(topk_p, axis=-1, keepdims=True) + EPS)
        gate = (xt @ w_gate).reshape(T, K, I)
        up = (xt @ w_up).reshape(T, K, I)
        basis = jax.nn.silu(gate) * up
        p = amplitudes[..., 0] ** 2 + amplitudes[..., 1] ** 2
        mix = p / (jnp.sum(p, axis=-1, keepdims=True) + EPS)
        mix_sel = mix[topk_idx]
        mixed = jnp.einsum('tek,tki->tei', mix_sel, basis)
        down = jnp.einsum('tei,ih->teh', mixed, w_down)
        coeff = topk_w * expert_scale[topk_idx]
        out = jnp.einsum('teh,te->th', down, coeff)
        shared = jax.nn.silu(xt @ shared_w_gate) * (xt @ shared_w_up) @ shared_w_down
        out = out + shared
        return out.reshape(B, S, H)
    x = x + _L0_xattn_ref(_layernorm(x, axis=-1), ctx_512, ctx_512, L0_xattn_Wc, L0_xattn_bc)
    x = x + _L0_ffn_ref(_layernorm(x, axis=-1), L0_ffn_w_router, L0_ffn_w_gate, L0_ffn_w_up, L0_ffn_w_down, L0_ffn_amplitudes, L0_ffn_expert_scale, L0_ffn_shared_w_gate, L0_ffn_shared_w_up, L0_ffn_shared_w_down)
    return x

_drawn_inputs = setup_inputs


def setup_inputs(seed=0):
    import zlib

    import numpy as np

    out = dict(_drawn_inputs(seed))
    spreads = {'L0_ffn_expert_scale': (1.0, 0.6)}
    factors = {'L0_ffn_w_router': 8.0,
     'L0_ffn_w_gate': 8.0,
     'L0_ffn_w_up': 8.0,
     'L0_ffn_w_down': 8.0,
     'L0_ffn_amplitudes': 8.0,
     'L0_ffn_shared_w_gate': 3.605,
     'L0_ffn_shared_w_up': 3.554,
     'L0_ffn_shared_w_down': 3.549}
    for name, (base, spread) in spreads.items():
        noise = np.random.default_rng([zlib.crc32(name.encode()), seed]).standard_normal(out[name].shape)
        drawn = base * np.exp(spread * noise) if base else spread * noise
        out[name] = jnp.asarray(drawn.astype(out[name].dtype))
    for name, factor in factors.items():
        out[name] = (out[name] * factor).astype(out[name].dtype)
    return out
```

```python
from contextlib import ExitStack

import concourse.bass as bass
from concourse import mybir

F32 = mybir.dt.float32
F32R = mybir.dt.float32r
ALU = mybir.AluOpType
ACT = mybir.ActivationFunctionType
AX = mybir.AxisListType

P = 128
HEADS = 16
GROUPS = 4
PER_GROUP = HEADS // GROUPS
DH = 16
VW = DH + 1
TOPK = 4
LN_EPS = 1e-5
FFN_EPS = 1e-8
SCORE_SCALE = DH ** -0.5
SPARE, TAKEN, BORDER = -3.0e38, -3.3e38, -3.2e38


def build(nc, x, ctx_in, wc, bc, w_router, w_gate, w_up, w_down, amplitudes, expert_scale,
          shared_gate, shared_up, shared_down, out):
    B, S, D = x.shape
    T = ctx_in.shape[1]
    DC = ctx_in.shape[2]
    E = w_router.shape[1]
    K = amplitudes.shape[1]
    I = w_down.shape[0]
    SI = shared_down.shape[0]
    assert (S, T, D, DC, E, I, SI, K) == (P, P, 2 * P, GROUPS * DH, P, P, 2 * P, 8)
    KC = D // P
    HALF_K = K // 2
    UP0, SG0, RT0 = K * I, 2 * K * I, 2 * K * I + 2 * SI
    WCOLS = RT0 + E
    WD0 = KC * WCOLS
    WALL = WD0 + 3 * D
    CONSTS = 3 + 8
    FIRST, LAST = 1, B - 4
    SPLIT = WALL // (LAST - FIRST + 1)
    assert SPLIT * (LAST - FIRST + 1) == WALL

    with ExitStack() as stack:
        def sb(name, shape, dt=F32):
            return stack.enter_context(nc.sbuf_tensor(name, shape, dt))

        def sem(name):
            return stack.enter_context(nc.semaphore(name))

        def two(name, shape, dt=F32):
            return [sb(f"{name}{n}", shape, dt) for n in range(2)]

        def f32(ap):
            return ap.bitcast(F32)

        rows = sb("rows", [P, B, D])
        ctx_sb = sb("ctx_sb", [P, B, DC])
        ident_f = sb("ident_f", [P, P])
        ident_r = sb("ident_r", [P, P], F32R)
        neg_half = sb("neg_half", [P, 1])
        wc_sb = sb("wc_sb", [P, 2, D])
        wcT_hi = sb("wcT_hi", [P, 2, D], F32R)
        wcT_lo = sb("wcT_lo", [P, 2, D], F32R)
        bias_bc = sb("bias_bc", [P, D])
        w_all = sb("w_all", [P, WALL])
        w_hi = sb("w_hi", [P, WALL], F32R)
        w_lo = sb("w_lo", [P, WALL], F32R)
        amp = sb("amp", [P, K, 2])
        amp_sq = sb("amp_sq", [P, K, 2])
        power = sb("power", [P, K])
        power_sum = sb("power_sum", [P, 1])
        power_den = sb("power_den", [P, 1])
        power_rec = sb("power_rec", [P, 1])
        escale = sb("escale", [P, 1])
        mix = sb("mix", [P, K])
        neg_sel_f = sb("neg_sel_f", [8, GROUPS, P])
        neg_sel = sb("neg_sel", [8, GROUPS, P], F32R)

        stats = two("stats", [P, 6])
        moments = two("moments", [P, 2])
        var_eps = two("var_eps", [P, 1])
        rstd = two("rstd", [P, 1])
        normed = two("normed", [P, D])
        x_bias = two("x_bias", [P, D])
        q_parts = two("q_parts", [P, 8, 2, 4 * DH], F32R)
        k_parts = two("k_parts", [P, 2, 2, 4 * DH], F32R)
        v_ones = two("v_ones", [P, GROUPS, VW])
        qT = two("qT", [P, 2, PER_GROUP, S], F32R)
        kT = two("kT", [P, 2, 2, T], F32R)
        row_max = two("row_max", [P, 2, PER_GROUP, 2])
        max_parts = two("max_parts", [P, PER_GROUP, 2, 2, 2], F32R)
        maxT = two("maxT", [8, PER_GROUP, S], F32R)
        probs = [sb(f"probs{u}", [P, PER_GROUP, S]) for u in range(GROUPS)]
        den_rec = two("den_rec", [P, HEADS])
        attn = two("attn", [P, HEADS, DH])
        attnT_hi = two("attnT_hi", [P, KC, S], F32R)
        attnT_lo = two("attnT_lo", [P, KC, S], F32R)

        yT_hi = two("yT_hi", [P, KC, S], F32R)
        yT_lo = two("yT_lo", [P, KC, S], F32R)
        logits = two("logits", [P, E + TOPK])
        top8 = two("top8", [P, 8])
        best4 = two("best4", [P, 8])
        neg_top = two("neg_top", [P, 1])
        replaced = two("replaced", [P, E + TOPK])
        expo = two("expo", [P, E])
        exp_sum = two("exp_sum", [P, 1])
        chosen = two("chosen", [P, E])
        chosen_sum = two("chosen_sum", [P, 1])
        coeff_den = two("coeff_den", [P, 1])
        coeff_rec = two("coeff_rec", [P, 1])
        chosenT = two("chosenT", [P, S])
        coeff = two("coeff", [P, K])
        tanh_g = two("tanh_g", [P, HALF_K * I])
        gated = two("gated", [P, HALF_K * I])
        bases = two("bases", [P, K, I])
        sum4 = sb("sum4", [P, 4, I])
        sum2 = sb("sum2", [P, 2, I])
        zsum = two("zsum", [P, I])
        tanh_s = sb("tanh_s", [P, SI])
        gated_s = sb("gated_s", [P, SI])
        shared = two("shared", [P, SI])
        hT_hi = two("hT_hi", [P, 3, S], F32R)
        hT_lo = two("hT_lo", [P, 3, S], F32R)
        out_sb = two("out_sb", [P, D])

        bank = [stack.enter_context(nc.psum_tensor(f"bank{n}", [P, 512], F32)) for n in range(8)]
        ps_qT, ps_max, ps_score = bank[0:2], bank[2:4], bank[4:6]
        ps_pv, ps_mixed = bank[6], bank[7]
        ps_y, ps_route, ps_gate, ps_up = bank[0], bank[1], bank[2:4], bank[4:6]
        ps_shared, ps_out = bank[6], bank[7]

        x_loaded = [sem(f"x_loaded{n}") for n in range(2)]
        ctx_loaded = [sem(f"ctx_loaded{n}") for n in range(2)]
        wc_loaded, bias_loaded = sem("wc_loaded"), sem("bias_loaded")
        amp_loaded, w_loaded = sem("amp_loaded"), sem("w_loaded")
        zeroed, ident_made, ident_r_made, consts_made = (
            sem("zeroed"), sem("ident_made"), sem("ident_r_made"), sem("consts_made"))
        wcT_ps, wcT_hi_made, wcT_made = sem("wcT_ps"), sem("wcT_hi_made"), sem("wcT_made")
        amp_step, w_split = sem("amp_step"), sem("w_split")
        stats_done, moments_done, var_done, rstd_done, normed_done = (
            sem("stats_done"), sem("moments_done"), sem("var_done"), sem("rstd_done"), sem("normed_done"))
        x_bias_done = sem("x_bias_done")
        q_hi_done, q_lo_done, k_hi_done, k_lo_done, v_done = (
            sem("q_hi_done"), sem("q_lo_done"), sem("k_hi_done"), sem("k_lo_done"), sem("v_done"))
        qT_ps, qT_done = sem("qT_ps"), sem("qT_done")
        kT_ps, kT_done = sem("kT_ps"), sem("kT_done")
        max_ps, max_done = sem("max_ps"), sem("max_done")
        max_hi_done, max_lo_done, maxT_ps, maxT_done = (
            sem("max_hi_done"), sem("max_lo_done"), sem("maxT_ps"), sem("maxT_done"))
        score_ps, probs_done, pv_ps = sem("score_ps"), sem("probs_done"), sem("pv_ps")
        den_rec_done, attn_done, attnT_ps, attnT_hi_done, attnT_lo_done, proj_ps, x1_done = (
            sem("den_rec_done"), sem("attn_done"), sem("attnT_ps"), sem("attnT_hi_done"),
            sem("attnT_lo_done"), sem("proj_ps"), sem("x1_done"))

        yT_ps, yT_hi_done, yT_lo_done = sem("yT_ps"), sem("yT_hi_done"), sem("yT_lo_done")
        route_ps, logits_done, top8_done, neg_top_done, best4_done = (
            sem("route_ps"), sem("logits_done"), sem("top8_done"), sem("neg_top_done"), sem("best4_done"))
        exp_done, replaced_done, chosen_done, coeff_den_done, coeff_rec_done = (
            sem("exp_done"), sem("replaced_done"), sem("chosen_done"), sem("coeff_den_done"),
            sem("coeff_rec_done"))
        chosenT_ps, chosenT_done, coeff_ps, coeff_done = (
            sem("chosenT_ps"), sem("chosenT_done"), sem("coeff_ps"), sem("coeff_done"))
        gate_ps, up_ps, tanh_done, gated_done, bases_done = (
            sem("gate_ps"), sem("up_ps"), sem("tanh_done"), sem("gated_done"), sem("bases_done"))
        sum_step, z_done = sem("sum_step"), sem("z_done")
        shared_ps, tanh_s_done, gated_s_done, shared_done = (
            sem("shared_ps"), sem("tanh_s_done"), sem("gated_s_done"), sem("shared_done"))
        hT_ps, hT_hi_done, hT_lo_done, out_ps, out_done = (
            sem("hT_ps"), sem("hT_hi_done"), sem("hT_lo_done"), sem("out_ps"), sem("out_done"))
        out_stored = [sem(f"out_stored{n}") for n in range(2)]

        block = stack.enter_context(nc.Block())

        def parity(b):
            return (FIRST + b[1]) % 2 if isinstance(b, tuple) else b % 2

        def at(b, per=1, plus=0):
            if isinstance(b, tuple):
                return b[0] * (2 * per) + (per * (FIRST + b[1]) + plus)
            return per * b + plus

        def by_parity(b):
            if isinstance(b, tuple):
                return b[0] * 16 + 16 * ((FIRST + b[1]) // 2 + 1)
            return 16 * (b // 2 + 1)

        def shift(b, by):
            return (b[0], b[1] + by) if isinstance(b, tuple) else b + by

        def row(t, b):
            if isinstance(b, tuple):
                return t[:, bass.ds(b[0] * 2 + (FIRST + b[1]), 1), :].rearrange("p a d -> p (a d)")
            return t[:, b, :]

        def keys_twice(b, a):
            c = row(ctx_sb, b)[:, 2 * DH * a:2 * DH * (a + 1)]
            return c.rearrange("p (r u d) -> p r u d", r=2, u=1).to_broadcast([P, 2, 2, DH])

        def heads_of(t):
            return t[:, :].rearrange("p (a t d) -> p a t d", a=2, d=DH)

        def q_place(n, part):
            return q_parts[n][:, :, :, part * DH:(part + 1) * DH].rearrange("p t a d -> p a t d")

        def group_of(u):
            return 2 * (u % 2) + u // 2

        def steps(eng, step):
            for b in range(FIRST):
                step(b, b)
            with eng.Fori(0, (LAST - FIRST + 1) // 2) as r:
                for n in range(2):
                    step((r, n), None)
            for b in range(LAST + 1, B):
                step(b, b)

        def has(n, by):
            return n is None or 0 <= n + by < B

        def wait(eng, s, b, per=1, plus=0, n=0):
            v = at(b, per, plus)
            if isinstance(b, tuple) or v > 0:
                eng.wait_ge(s, v)

        def wait_alone(eng, s, v):
            if not isinstance(v, int):
                v = eng.to_reg(v)
            eng.wait_ge(consts_made, CONSTS)
            if not isinstance(v, int) or v > 0:
                eng.wait_ge(s, v)

        @block.sync
        def _(sp):
            def load(b):
                n = parity(b)
                sp.dma_start(row(rows, b), dram_row(x, b)).then_inc(x_loaded[n], 16)
                sp.dma_start(row(ctx_sb, b), dram_row(ctx_in, b)).then_inc(ctx_loaded[n], 16)

            def dram_row(t, b):
                if isinstance(b, tuple):
                    return t[bass.ds(b[0] * 2 + (FIRST + b[1]), 1), :, :].rearrange("a p d -> (a p) d")
                return t[b]

            for b in range(2):
                load(b)
            sp.dma_start(wc_sb[:, :, :], wc.rearrange("(m p) d -> p m d", p=P)).then_inc(wc_loaded, 16)
            for b in range(2, FIRST + 2):
                sp.wait_ge(x_loaded[b % 2], 16 * (b // 2))
                sp.wait_ge(ctx_loaded[b % 2], 16 * (b // 2))
                load(b)
            with sp.Fori(0, (LAST - FIRST + 1) // 2) as r:
                for n in range(2):
                    ahead, before = (r, n + 2), (r, n)
                    sp.wait_ge(x_loaded[parity(before)], by_parity(before))
                    sp.wait_ge(ctx_loaded[parity(before)], by_parity(before))
                    load(ahead)
            for b in range(LAST + 3, B):
                sp.wait_ge(x_loaded[b % 2], 16 * (b // 2))
                sp.wait_ge(ctx_loaded[b % 2], 16 * (b // 2))
                load(b)

            def store(b, n):
                sp.wait_ge(out_done, at(b, 1, 1))
                if isinstance(b, tuple):
                    dst = out[bass.ds(b[0] * 2 + (FIRST + b[1]), 1), :, :].rearrange("a p d -> (a p) d")
                else:
                    dst = out[b]
                sp.dma_start(dst, out_sb[parity(b)][:, :]).then_inc(out_stored[parity(b)], 16)

            steps(sp, store)
            for n in range(2):
                sp.wait_ge(out_stored[n], 16 * (B // 2))

        @block.gpsimd
        def _(pool):
            nc.gpsimd.memset(ident_f[:, :], 0.0).then_inc(zeroed, 1)
            pool.wait_ge(zeroed, 1)
            nc.gpsimd.affine_select(out=ident_f[:, :], in_=ident_f[:, :], compare_op=ALU.not_equal,
                                    fill=1.0, base=0, pattern=[[-1, P]],
                                    channel_multiplier=1).then_inc(ident_made, 1)
            nc.gpsimd.memset(neg_half[:, :], -0.5).then_inc(consts_made, 1)
            nc.gpsimd.memset(neg_sel_f[:, :, :], 0.0).then_inc(zeroed, 1)
            pool.wait_ge(zeroed, 2)
            for part in range(2):
                nc.gpsimd.affine_select(out=neg_sel_f[:, :, :], in_=neg_sel_f[:, :, :],
                                        compare_op=ALU.not_equal, fill=-1.0, base=-part,
                                        pattern=[[-2, GROUPS], [0, P]],
                                        channel_multiplier=1).then_inc(consts_made, 1)
                pool.wait_ge(consts_made, 2 + part)
            for n in range(2):
                nc.gpsimd.memset(f32(kT[n][:, :, :, :]), 0.0).then_inc(consts_made, 1)
                nc.gpsimd.memset(v_ones[n][:, :, DH:VW], 1.0).then_inc(consts_made, 1)
                nc.gpsimd.memset(logits[n][:, E:E + TOPK], SPARE).then_inc(consts_made, 1)
                nc.gpsimd.memset(best4[n][:, TOPK:8], SPARE).then_inc(consts_made, 1)
            w_view = w_all[:, 0:WD0].rearrange("p (c n) -> p c n", c=KC)
            for src, c0 in ((w_gate, 0), (w_up, UP0), (shared_gate, SG0), (shared_up, SG0 + SI),
                            (w_router, RT0)):
                pool.dma_start(w_view[:, :, c0:c0 + src.shape[1]],
                               src.rearrange("(c p) n -> p c n", p=P)).then_inc(w_loaded, 16)
            pool.dma_start(w_all[:, WD0:WD0 + D], w_down).then_inc(w_loaded, 16)
            pool.dma_start(w_all[:, WD0 + D:WALL].rearrange("p (c n) -> p c n", c=2),
                           shared_down.rearrange("(c p) n -> p c n", p=P)).then_inc(w_loaded, 16)

            def rsqrt(b, plus=0):
                n = parity(b)
                pool.wait_ge(var_done, at(b, 1, 1 + plus))
                nc.gpsimd.tensor_tensor(rstd[n][:, :], var_eps[n][:, :], neg_half[:, :],
                                        ALU.pow).then_inc(rstd_done, 1)

            def add_bias(b):
                n = parity(b)
                pool.wait_ge(x_loaded[n], by_parity(b))
                wait(pool, x1_done, b, 1, -1)
                nc.gpsimd.tensor_tensor(x_bias[n][:, :], row(rows, b), bias_bc[:, :],
                                        ALU.add).then_inc(x_bias_done, 1)

            def split_weights(b):
                if not isinstance(b, tuple):
                    return
                c = bass.ds(b[0] * (2 * SPLIT) + b[1] * SPLIT, SPLIT)
                nc.gpsimd.tensor_copy(w_hi[:, c], w_all[:, c]).then_inc(w_split, 1)
                pool.wait_ge(w_split, b[0] * 4 + (2 * b[1] + 1))
                nc.gpsimd.tensor_tensor(w_lo[:, c], w_all[:, c], f32(w_hi[:, c]),
                                        ALU.subtract).then_inc(w_split, 1)

            rsqrt(0)
            rsqrt(1)
            pool.wait_ge(bias_loaded, 16)
            pool.wait_ge(w_loaded, 16 * 7)

            def step(b, n):
                if has(n, 2):
                    rsqrt(shift(b, 2))
                add_bias(b)
                split_weights(b)

            steps(pool, step)

            def sum_bases(b):
                n = parity(b)
                pool.wait_ge(bases_done, at(b, 2, 2))
                nc.gpsimd.tensor_tensor(sum4[:, :, :], bases[n][:, 0:4, :], bases[n][:, 4:8, :],
                                        ALU.add).then_inc(sum_step, 1)
                pool.wait_ge(sum_step, at(b, 2, 1))
                nc.gpsimd.tensor_tensor(sum2[:, :, :], sum4[:, 0:2, :], sum4[:, 2:4, :],
                                        ALU.add).then_inc(sum_step, 1)
                pool.wait_ge(sum_step, at(b, 2, 2))
                wait(pool, hT_ps, b, 1, -1)
                nc.gpsimd.tensor_tensor(zsum[n][:, :], sum2[:, 0, :], sum2[:, 1, :],
                                        ALU.add).then_inc(z_done, 1)

            rsqrt(0, B)
            rsqrt(1, B)

            def step2(b, n):
                if has(n, 2):
                    rsqrt(shift(b, 2), B)
                sum_bases(b)

            steps(pool, step2)

        @block.scalar
        def _(act):
            act.dma_start(bias_bc[:, :], bc.rearrange("(a d) -> a d", a=1).to_broadcast([P, D])
                          if False else bc.partition_broadcast(P)).then_inc(bias_loaded, 16)
            act.dma_start(amp[:, :, :], amplitudes).then_inc(amp_loaded, 16)
            act.dma_start(escale[:, :], expert_scale.rearrange("(e a) -> e a", a=1)).then_inc(amp_loaded, 16)

            def keys(b):
                n = parity(b)
                act.wait_ge(ctx_loaded[n], by_parity(b))
                wait_alone(act, kT_ps, at(b, 1, -1))
                for a in range(2):
                    t = nc.scalar.activation(
                        k_parts[n][:, :, a, 0:2 * DH].rearrange("p r (u d) -> p r u d", u=2),
                        keys_twice(b, a), ACT.Copy)
                t.then_inc(k_hi_done, 1)

            def values(b):
                n = parity(b)
                wait_alone(act, pv_ps, at(b, 4, -4))
                nc.scalar.activation(v_ones[n][:, :, 0:DH], row(ctx_sb, b).rearrange("p (g d) -> p g d", g=GROUPS),
                                     ACT.Copy).then_inc(v_done, 1)

            def q_hi(b):
                n = parity(b)
                act.wait_ge(normed_done, at(b, 1, 1))
                wait(act, qT_ps, b, 2, -2)
                for u in range(2):
                    t = nc.scalar.activation(q_place(n, 2 * u), heads_of(normed[n]), ACT.Copy)
                t.then_inc(q_hi_done, 1)

            def evacuate_qT_kT(b):
                n = parity(b)
                wait(act, score_ps, b, 4, -4)
                for pair in range(2):
                    act.wait_ge(qT_ps, at(b, 2, pair + 1))
                    nc.scalar.activation(qT[n][:, pair, :, :].rearrange("p j s -> p (j s)"),
                                         ps_qT[pair][:, :], ACT.Copy).then_inc(qT_done, 1)
                act.wait_ge(kT_ps, at(b, 1, 1))
                src = ps_mixed[:, 0:2 * T].rearrange("p (a t) -> p a t", a=2)
                nc.scalar.activation(kT[n][0:64, :, 0, :], src[0:64, :, :], ACT.Copy)
                nc.scalar.activation(kT[n][64:128, :, 1, :], src[64:128, :, :], ACT.Copy).then_inc(kT_done, 1)

            def evacuate_maxT(b):
                n = parity(b)
                act.wait_ge(maxT_ps, at(b, 1, 1))
                wait(act, score_ps, b, 4, -4)
                nc.scalar.activation(maxT[n][:, :, :].rearrange("p j s -> p (j s)"),
                                     ps_mixed[0:8, :], ACT.Copy).then_inc(maxT_done, 1)

            def exps(b, u):
                act.wait_ge(score_ps, at(b, 4, u + 1))
                wait(act, pv_ps, b, 4, u - 3)
                nc.scalar.activation(probs[u][:, :, :].rearrange("p j s -> p (j s)"), ps_score[u % 2][:, :],
                                     ACT.Exp, scale=SCORE_SCALE).then_inc(probs_done, 1)

            def attnT(b):
                n = parity(b)
                act.wait_ge(attnT_ps, at(b, 1, 1))
                nc.scalar.activation(attnT_hi[n][:, :, :].rearrange("p c s -> p (c s)"),
                                     ps_mixed[:, 0:KC * S], ACT.Copy).then_inc(attnT_hi_done, 1)

            act.wait_ge(consts_made, CONSTS)
            keys(0)
            values(0)
            keys(1)
            q_hi(0)
            act.wait_ge(wcT_ps, 1)
            nc.scalar.activation(wcT_hi[:, :, :].rearrange("p c n -> p (c n)"), ps_score[0][:, :],
                                 ACT.Copy).then_inc(wcT_hi_made, 1)
            evacuate_qT_kT(0)
            q_hi(1)

            def step(b, n):
                evacuate_maxT(b)
                if has(n, 1):
                    evacuate_qT_kT(shift(b, 1))
                exps(b, 0)
                exps(b, 1)
                if has(n, -1):
                    attnT(shift(b, -1))
                exps(b, 2)
                if has(n, 1):
                    values(shift(b, 1))
                if has(n, 2):
                    keys(shift(b, 2))
                exps(b, 3)
                if has(n, 2):
                    q_hi(shift(b, 2))

            steps(act, step)
            attnT(B - 1)

            def yT(b):
                n = parity(b)
                act.wait_ge(yT_ps, at(b, 1, 1))
                wait(act, shared_ps, b, 1, -1)
                nc.scalar.activation(yT_hi[n][:, :, :].rearrange("p c s -> p (c s)"),
                                     ps_y[:, 0:KC * S], ACT.Copy).then_inc(yT_hi_done, 1)

            def copy_logits(b):
                n = parity(b)
                act.wait_ge(route_ps, at(b, 1, 1))
                wait(act, replaced_done, b, 1, -1)
                nc.scalar.activation(logits[n][:, 0:E], ps_route[:, 0:E], ACT.Copy).then_inc(logits_done, 1)

            def exp_logits(b):
                n = parity(b)
                act.wait_ge(neg_top_done, at(b, 1, 1))
                wait(act, coeff_den_done, b, 1, -1)
                nc.scalar.activation(expo[n][:, :], logits[n][:, 0:E], ACT.Exp, bias=neg_top[n][:, 0:1],
                                     accum_out=exp_sum[n][:, 0:1]).then_inc(exp_done, 1)

            def copy_chosenT(b):
                n = parity(b)
                act.wait_ge(chosenT_ps, at(b, 1, 1))
                wait(act, coeff_ps, b, 1, -1)
                nc.scalar.activation(chosenT[n][:, :], ps_route[:, E:E + S], ACT.Copy).then_inc(chosenT_done, 1)

            def tanh(b, half):
                act.wait_ge(gate_ps, at(b, 2, half + 1))
                wait(act, gated_done, b, 2, half - 1)
                nc.scalar.activation(tanh_g[half][:, :], ps_gate[half][:, :], ACT.Tanh,
                                     scale=0.5).then_inc(tanh_done, 1)

            def tanh_shared(b):
                act.wait_ge(shared_ps, at(b, 1, 1))
                wait(act, gated_s_done, b, 1, 0)
                nc.scalar.activation(tanh_s[:, :], ps_shared[:, 0:SI], ACT.Tanh,
                                     scale=0.5).then_inc(tanh_s_done, 1)

            def hT(b):
                n = parity(b)
                act.wait_ge(hT_ps, at(b, 1, 1))
                nc.scalar.activation(hT_hi[n][:, :, :].rearrange("p c s -> p (c s)"), ps_out[:, 0:3 * S],
                                     ACT.Copy, scale=0.5).then_inc(hT_hi_done, 1)

            def route_a(b):
                copy_logits(b)
                exp_logits(b)

            yT(0)
            route_a(0)
            copy_chosenT(0)

            def step2(b, n):
                if has(n, 1):
                    yT(shift(b, 1))
                tanh(b, 0)
                if has(n, 1):
                    route_a(shift(b, 1))
                tanh(b, 1)
                if has(n, -1):
                    hT(shift(b, -1))
                if has(n, 1):
                    copy_chosenT(shift(b, 1))
                tanh_shared(b)

            steps(act, step2)
            hT(B - 1)

        @block.tensor
        def _(pe):
            def transpose_q(b):
                n = parity(b)
                pe.wait_ge(q_lo_done, at(b, 1, 1))
                for pair in range(2):
                    wait(pe, qT_done, b, 2, pair - 1)
                    for j in range(PER_GROUP):
                        src = q_parts[n][:, PER_GROUP * pair + j, :, :].rearrange("p a d -> p (a d)")
                        t = nc.tensor.transpose(ps_qT[pair][:, j * S:(j + 1) * S].bitcast(F32R), src,
                                                ident_r[:, :])
                    t.then_inc(qT_ps, 1)

            def transpose_k(b):
                n = parity(b)
                pe.wait_ge(k_lo_done, at(b, 1, 1))
                wait(pe, maxT_done, b)
                for pair in range(2):
                    t = nc.tensor.transpose(ps_mixed[:, pair * T:(pair + 1) * T].bitcast(F32R),
                                            k_parts[n][:, pair, :, :].rearrange("p a d -> p (a d)"),
                                            ident_r[:, :])
                t.then_inc(kT_ps, 1)

            def max_scores(b, part):
                n, pair = parity(b), part // 2
                pe.wait_ge(qT_done, at(b, 2, pair + 1))
                pe.wait_ge(kT_done, at(b, 1, 1))
                wait(pe, max_done, b, 4, part - 1)
                for u in range(2):
                    t = nc.tensor.matmul(ps_max[part % 2][:, 2 * T * u:2 * T * (u + 1)],
                                         qT[n][:, pair, 2 * (part % 2) + u, :],
                                         kT[n][:, pair, :, :].rearrange("p a t -> p (a t)"),
                                         start=True, stop=True)
                t.then_inc(max_ps, 1)

            def transpose_max(b):
                n = parity(b)
                pe.wait_ge(max_lo_done, at(b, 1, 1))
                wait(pe, x1_done, b, 1, -1)
                for j in range(PER_GROUP):
                    t = nc.tensor.transpose(ps_mixed[0:8, j * S:(j + 1) * S].bitcast(F32R),
                                            max_parts[n][:, j, :, :, :].rearrange("p a b c -> p (a b c)"),
                                            ident_r[:, :])
                t.then_inc(maxT_ps, 1)

            def scores(b, u):
                n, pair, a = parity(b), u // 2, u % 2
                pe.wait_ge(maxT_done, at(b, 1, 1))
                wait(pe, probs_done, b, 4, u - 1)
                nc.tensor.matmul(ps_score[u % 2][:, :], kT[n][64 * a:64 * a + 64, pair, a, :],
                                 qT[n][64 * a:64 * a + 64, pair, :, :].rearrange("p j s -> p (j s)"),
                                 start=True, stop=False)
                nc.tensor.matmul(ps_score[u % 2][:, :], neg_sel[:, u, :],
                                 maxT[n][:, :, :].rearrange("p j s -> p (j s)"),
                                 start=False, stop=True).then_inc(score_ps, 1)

            def values(b, u):
                pe.wait_ge(probs_done, at(b, 4, u + 1))
                g = group_of(u)
                if u == 0:
                    pe.wait_ge(v_done, at(b, 1, 1))
                    wait(pe, attn_done, b)
                for j in range(PER_GROUP):
                    h = PER_GROUP * g + j
                    t = nc.tensor.matmul(ps_pv[:, h * VW:(h + 1) * VW], probs[u][:, j, :],
                                         v_ones[parity(b)][:, g, :], start=True, stop=True)
                t.then_inc(pv_ps, 1)

            def transpose_attn(b):
                n = parity(b)
                pe.wait_ge(attn_done, at(b, 1, 1))
                for c in range(KC):
                    t = nc.tensor.transpose(ps_mixed[:, c * S:(c + 1) * S],
                                            attn[n][:, 8 * c:8 * c + 8, :].rearrange("p h d -> p (h d)"),
                                            ident_f[:, :])
                t.then_inc(attnT_ps, 1)

            def three_passes(dst, hi, lo, rhs_hi, rhs_lo, chunks):
                k = 0
                for c in range(chunks):
                    for l, r in ((hi, rhs_hi), (hi, rhs_lo), (lo, rhs_hi)):
                        t = nc.tensor.matmul(dst, l(c), r(c), start=(k == 0), stop=(k == 3 * chunks - 1))
                        k += 1
                return t

            def project(b):
                n = parity(b)
                pe.wait_ge(attnT_lo_done, at(b, 1, 1))
                three_passes(ps_mixed[:, 0:D], lambda c: attnT_hi[n][:, c, :], lambda c: attnT_lo[n][:, c, :],
                             lambda c: wcT_hi[:, c, :], lambda c: wcT_lo[:, c, :], KC).then_inc(proj_ps, 1)

            pe.wait_ge(ident_made, 1)
            pe.wait_ge(wc_loaded, 16)
            for c in range(KC):
                for m in range(2):
                    t = nc.tensor.transpose(ps_score[0][:, c * D + m * P:c * D + (m + 1) * P],
                                            wc_sb[:, m, c * P:(c + 1) * P], ident_f[:, :])
            t.then_inc(wcT_ps, 1)
            pe.wait_ge(ident_r_made, 2)
            transpose_q(0)
            transpose_k(0)
            for part in range(4):
                max_scores(0, part)
            pe.wait_ge(wcT_made, 1)

            def step(b, n):
                transpose_max(b)
                if has(n, 1):
                    transpose_q(shift(b, 1))
                    transpose_k(shift(b, 1))
                scores(b, 0)
                scores(b, 1)
                if has(n, -1):
                    if has(n, 1):
                        pe.wait_ge(kT_done, at(b, 1, 2))
                    transpose_attn(shift(b, -1))
                values(b, 0)
                if has(n, 1):
                    max_scores(shift(b, 1), 0)
                    max_scores(shift(b, 1), 1)
                scores(b, 2)
                values(b, 1)
                if has(n, 1):
                    max_scores(shift(b, 1), 2)
                    max_scores(shift(b, 1), 3)
                scores(b, 3)
                if has(n, -1):
                    project(shift(b, -1))
                values(b, 2)
                values(b, 3)

            steps(pe, step)
            transpose_attn(B - 1)
            project(B - 1)

            def transpose_y(b):
                n = parity(b)
                pe.wait_ge(normed_done, at(b, 1, B + 1))
                wait(pe, yT_lo_done, b)
                for c in range(KC):
                    t = nc.tensor.transpose(ps_y[:, c * S:(c + 1) * S], normed[n][:, c * P:(c + 1) * P],
                                            ident_f[:, :])
                t.then_inc(yT_ps, 1)

            def weights(b, dst, c0, width):
                n = parity(b)
                return three_passes(dst, lambda c: yT_hi[n][:, c, :], lambda c: yT_lo[n][:, c, :],
                                    lambda c: w_hi[:, c * WCOLS + c0:c * WCOLS + c0 + width],
                                    lambda c: w_lo[:, c * WCOLS + c0:c * WCOLS + c0 + width], KC)

            def route(b):
                pe.wait_ge(yT_lo_done, at(b, 1, 1))
                wait(pe, coeff_done, b)
                weights(b, ps_route[:, 0:E], RT0, E).then_inc(route_ps, 1)

            def transpose_chosen(b):
                pe.wait_ge(chosen_done, at(b, 1, 1))
                nc.tensor.transpose(ps_route[:, E:E + S], chosen[parity(b)][:, :],
                                    ident_f[:, :]).then_inc(chosenT_ps, 1)

            def mix_experts(b):
                pe.wait_ge(chosenT_done, at(b, 1, 1))
                nc.tensor.matmul(ps_route[:, E + S:E + S + K], chosenT[parity(b)][:, :], mix[:, :],
                                 start=True, stop=True).then_inc(coeff_ps, 1)

            def gate(b, half):
                wait(pe, bases_done, b, 2, half - 1)
                weights(b, ps_gate[half][:, :], half * HALF_K * I, HALF_K * I).then_inc(gate_ps, 1)

            def up(b, half):
                weights(b, ps_up[half][:, :], UP0 + half * HALF_K * I, HALF_K * I).then_inc(up_ps, 1)

            def shared_in(b):
                wait(pe, shared_done, b)
                weights(b, ps_shared[:, :], SG0, 2 * SI).then_inc(shared_ps, 1)

            def transpose_h(b):
                n = parity(b)
                pe.wait_ge(z_done, at(b, 1, 1))
                pe.wait_ge(shared_done, at(b, 1, 1))
                wait(pe, out_done, b)
                nc.tensor.transpose(ps_out[:, 0:S], zsum[n][:, :], ident_f[:, :])
                for c in range(2):
                    t = nc.tensor.transpose(ps_out[:, (c + 1) * S:(c + 2) * S], shared[n][:, c * P:(c + 1) * P],
                                            ident_f[:, :])
                t.then_inc(hT_ps, 1)

            def down(b):
                n = parity(b)
                pe.wait_ge(hT_lo_done, at(b, 1, 1))
                three_passes(ps_out[:, 0:D], lambda c: hT_hi[n][:, c, :], lambda c: hT_lo[n][:, c, :],
                             lambda c: w_hi[:, WD0 + c * D:WD0 + (c + 1) * D],
                             lambda c: w_lo[:, WD0 + c * D:WD0 + (c + 1) * D], 3).then_inc(out_ps, 1)

            pe.wait_ge(w_split, 2 * (LAST - FIRST + 1))
            pe.wait_ge(amp_step, 6)
            transpose_y(0)
            pe.wait_ge(x1_done, B)
            route(0)
            transpose_chosen(0)
            mix_experts(0)

            def step2(b, n):
                if has(n, 1):
                    transpose_y(shift(b, 1))
                gate(b, 0)
                up(b, 0)
                if has(n, 1):
                    route(shift(b, 1))
                gate(b, 1)
                if has(n, -1):
                    transpose_h(shift(b, -1))
                up(b, 1)
                if has(n, 1):
                    transpose_chosen(shift(b, 1))
                if has(n, -1):
                    down(shift(b, -1))
                shared_in(b)
                if has(n, 1):
                    mix_experts(shift(b, 1))

            steps(pe, step2)
            transpose_h(B - 1)
            down(B - 1)

        @block.vector
        def _(dve):
            def moments_of(b, plus=0):
                n = parity(b)
                if plus:
                    dve.wait_ge(x1_done, at(b, 1, 1))
                else:
                    dve.wait_ge(x_loaded[n], by_parity(b))
                nc.vector.bn_stats(stats[n][:, :], row(rows, b)).then_inc(stats_done, 1)
                wait_alone(dve, stats_done, at(b, 1, 1 + plus))
                nc.vector.bn_aggr(moments[n][:, :], stats[n][:, :]).then_inc(moments_done, 1)
                dve.wait_ge(moments_done, at(b, 1, 1 + plus))
                nc.vector.tensor_scalar(var_eps[n][:, :], moments[n][:, 1:2], LN_EPS, None,
                                        ALU.add).then_inc(var_done, 1)

            def normalize(b, plus=0):
                n = parity(b)
                dve.wait_ge(rstd_done, at(b, 1, 1 + plus))
                if plus:
                    wait(dve, yT_ps, b, 1, -1)
                nc.vector.tensor_scalar(normed[n][:, :], row(rows, b), moments[n][:, 0:1], rstd[n][:, 0:1],
                                        ALU.subtract, ALU.mult).then_inc(normed_done, 1)

            def k_lo(b):
                n = parity(b)
                dve.wait_ge(k_hi_done, at(b, 1, 1))
                for a in range(2):
                    hi, lo = (k_parts[n][:, :, a, c:c + 2 * DH].rearrange("p r (u d) -> p r u d", u=2)
                              for c in (0, 2 * DH))
                    t = nc.vector.tensor_tensor(lo, keys_twice(b, a), f32(hi), ALU.subtract)
                t.then_inc(k_lo_done, 1)

            def q_lo(b):
                n = parity(b)
                dve.wait_ge(q_hi_done, at(b, 1, 1))
                for u in range(2):
                    t = nc.vector.tensor_tensor(q_place(n, 2 * u + 1), heads_of(normed[n]),
                                                f32(q_place(n, 2 * u)), ALU.subtract)
                t.then_inc(q_lo_done, 1)

            def maxima(b, part):
                n = parity(b)
                dve.wait_ge(max_ps, at(b, 4, part + 1))
                dst = row_max[n][:, part // 2, 2 * (part % 2):2 * (part % 2) + 2, :].rearrange("p j a -> p (j a)")
                nc.vector.tensor_reduce(dst, ps_max[part % 2][:, :].rearrange("p (x t) -> p x t", t=T),
                                        AX.X, ALU.max).then_inc(max_done, 1)

            def split_max(b):
                n = parity(b)
                dve.wait_ge(max_done, at(b, 4, 4))
                wait(dve, maxT_ps, b, 1, -1)
                view = max_parts[n][:, :, :, :, :].rearrange("p j r a c -> p r j a c")
                nc.vector.tensor_copy(view[:, :, :, :, 0], row_max[n][:, :, :, :]).then_inc(max_hi_done, 1)
                dve.wait_ge(max_hi_done, at(b, 1, 1))
                nc.vector.tensor_tensor(view[:, :, :, :, 1], row_max[n][:, :, :, :], f32(view[:, :, :, :, 0]),
                                        ALU.subtract).then_inc(max_lo_done, 1)

            def divide(b):
                n = parity(b)
                dve.wait_ge(pv_ps, at(b, 4, 4))
                pv = ps_pv[:, 0:HEADS * VW].rearrange("p (h w) -> p h w", w=VW)
                nc.vector.reciprocal(den_rec[n][:, :], pv[:, :, DH]).then_inc(den_rec_done, 1)
                dve.wait_ge(den_rec_done, at(b, 1, 1))
                nc.vector.tensor_tensor(
                    attn[n][:, :, :], pv[:, :, 0:DH],
                    den_rec[n][:, :].rearrange("p (h a) -> p h a", a=1).to_broadcast([P, HEADS, DH]),
                    ALU.mult).then_inc(attn_done, 1)

            def attnT(b):
                n = parity(b)
                dve.wait_ge(attnT_hi_done, at(b, 1, 1))
                nc.vector.tensor_tensor(attnT_lo[n][:, :, :].rearrange("p c s -> p (c s)"), ps_mixed[:, 0:KC * S],
                                        f32(attnT_hi[n][:, :, :]).rearrange("p c s -> p (c s)"),
                                        ALU.subtract).then_inc(attnT_lo_done, 1)

            def residual(b):
                n = parity(b)
                dve.wait_ge(proj_ps, at(b, 1, 1))
                dve.wait_ge(x_bias_done, at(b, 1, 1))
                nc.vector.tensor_tensor(row(rows, b), ps_mixed[:, 0:D], x_bias[n][:, :],
                                        ALU.add).then_inc(x1_done, 1)

            dve.wait_ge(ident_made, 1)
            nc.vector.tensor_copy(ident_r[:, :], ident_f[:, :]).then_inc(ident_r_made, 1)
            moments_of(0)
            moments_of(1)
            dve.wait_ge(consts_made, 3)
            nc.vector.tensor_copy(neg_sel[:, :, :], neg_sel_f[:, :, :]).then_inc(ident_r_made, 1)
            normalize(0)
            k_lo(0)
            q_lo(0)
            normalize(1)
            dve.wait_ge(wcT_hi_made, 1)
            nc.vector.tensor_tensor(wcT_lo[:, :, :].rearrange("p c n -> p (c n)"), ps_score[0][:, :],
                                    f32(wcT_hi[:, :, :]).rearrange("p c n -> p (c n)"),
                                    ALU.subtract).then_inc(wcT_made, 1)
            for part in range(4):
                maxima(0, part)
            split_max(0)
            k_lo(1)
            q_lo(1)
            dve.wait_ge(amp_loaded, 32)
            nc.vector.tensor_tensor(amp_sq[:, :, :], amp[:, :, :], amp[:, :, :], ALU.mult).then_inc(amp_step, 1)
            dve.wait_ge(amp_step, 1)
            nc.vector.tensor_reduce(power[:, :], amp_sq[:, :, :], AX.X, ALU.add).then_inc(amp_step, 1)
            dve.wait_ge(amp_step, 2)
            nc.vector.tensor_reduce(power_sum[:, :], power[:, :], AX.X, ALU.add).then_inc(amp_step, 1)
            dve.wait_ge(amp_step, 3)
            nc.vector.tensor_scalar(power_den[:, :], power_sum[:, :], FFN_EPS, None, ALU.add).then_inc(amp_step, 1)
            dve.wait_ge(amp_step, 4)
            nc.vector.reciprocal(power_rec[:, :], power_den[:, :]).then_inc(amp_step, 1)
            dve.wait_ge(amp_step, 5)
            nc.vector.tensor_scalar(mix[:, :], power[:, :], power_rec[:, 0:1], escale[:, 0:1],
                                    ALU.mult, ALU.mult).then_inc(amp_step, 1)

            def step(b, n):
                if has(n, -1):
                    divide(shift(b, -1))
                if has(n, 2):
                    moments_of(shift(b, 2))
                if has(n, -1):
                    attnT(shift(b, -1))
                if has(n, 1):
                    maxima(shift(b, 1), 0)
                    maxima(shift(b, 1), 1)
                if has(n, 2):
                    normalize(shift(b, 2))
                    k_lo_first = shift(b, 2)
                if has(n, 1):
                    maxima(shift(b, 1), 2)
                    maxima(shift(b, 1), 3)
                    split_max(shift(b, 1))
                if has(n, -1):
                    residual(shift(b, -1))
                if has(n, 2):
                    k_lo(k_lo_first)
                    q_lo(k_lo_first)

            steps(dve, step)
            moments_of(0, B)
            divide(B - 1)
            normalize(0, B)
            moments_of(1, B)
            attnT(B - 1)
            normalize(1, B)
            residual(B - 1)

            def yT(b):
                n = parity(b)
                dve.wait_ge(yT_hi_done, at(b, 1, 1))
                nc.vector.tensor_tensor(yT_lo[n][:, :, :].rearrange("p c s -> p (c s)"), ps_y[:, 0:KC * S],
                                        f32(yT_hi[n][:, :, :]).rearrange("p c s -> p (c s)"),
                                        ALU.subtract).then_inc(yT_lo_done, 1)

            def choose(b):
                n = parity(b)
                wait_alone(dve, logits_done, at(b, 1, 1))
                nc.vector.max(top8[n][:, :], logits[n][:, 0:E]).then_inc(top8_done, 1)
                dve.wait_ge(top8_done, at(b, 1, 1))
                nc.vector.tensor_scalar(neg_top[n][:, :], top8[n][:, 0:1], -1.0, None,
                                        ALU.mult).then_inc(neg_top_done, 1)
                nc.vector.tensor_copy(best4[n][:, 0:TOPK], top8[n][:, 0:TOPK]).then_inc(best4_done, 1)
                wait_alone(dve, best4_done, at(b, 1, 1))
                nc.vector.match_replace(replaced[n][:, :], best4[n][:, :], logits[n][:, :],
                                        TAKEN).then_inc(replaced_done, 1)
                dve.wait_ge(replaced_done, at(b, 1, 1))
                dve.wait_ge(exp_done, at(b, 1, 1))
                wait(dve, chosenT_ps, b, 1, -1)
                nc.vector.scalar_tensor_tensor(out=chosen[n][:, :], in0=replaced[n][:, 0:E], scalar=BORDER,
                                               in1=expo[n][:, :], op0=ALU.is_lt, op1=ALU.mult,
                                               accum_out=chosen_sum[n][:, 0:1]).then_inc(chosen_done, 1)
                dve.wait_ge(chosen_done, at(b, 1, 1))
                nc.vector.tensor_scalar(coeff_den[n][:, :], exp_sum[n][:, :], FFN_EPS, chosen_sum[n][:, 0:1],
                                        ALU.mult, ALU.add).then_inc(coeff_den_done, 1)
                dve.wait_ge(coeff_den_done, at(b, 1, 1))
                nc.vector.reciprocal(coeff_rec[n][:, :], coeff_den[n][:, :]).then_inc(coeff_rec_done, 1)

            def weigh(b):
                n = parity(b)
                dve.wait_ge(coeff_ps, at(b, 1, 1))
                dve.wait_ge(coeff_rec_done, at(b, 1, 1))
                nc.vector.tensor_scalar(coeff[n][:, :], ps_route[:, E + S:E + S + K], coeff_rec[n][:, 0:1], None,
                                        ALU.mult).then_inc(coeff_done, 1)

            def gate(b, half):
                dve.wait_ge(tanh_done, at(b, 2, half + 1))
                nc.vector.scalar_tensor_tensor(out=gated[half][:, :], in0=tanh_g[half][:, :], scalar=1.0,
                                               in1=ps_gate[half][:, :], op0=ALU.add,
                                               op1=ALU.mult).then_inc(gated_done, 1)

            def basis(b, half):
                n = parity(b)
                dve.wait_ge(gated_done, at(b, 2, half + 1))
                dve.wait_ge(up_ps, at(b, 2, half + 1))
                dve.wait_ge(coeff_done, at(b, 1, 1))
                wait(dve, z_done, b, 1, -1)
                for k in range(HALF_K):
                    t = nc.vector.scalar_tensor_tensor(
                        out=bases[n][:, half * HALF_K + k, :], in0=ps_up[half][:, k * I:(k + 1) * I],
                        scalar=coeff[n][:, half * HALF_K + k:half * HALF_K + k + 1],
                        in1=gated[half][:, k * I:(k + 1) * I], op0=ALU.mult, op1=ALU.mult)
                t.then_inc(bases_done, 1)

            def shared_basis(b):
                n = parity(b)
                dve.wait_ge(tanh_s_done, at(b, 1, 1))
                nc.vector.scalar_tensor_tensor(out=gated_s[:, :], in0=tanh_s[:, :], scalar=1.0,
                                               in1=ps_shared[:, 0:SI], op0=ALU.add,
                                               op1=ALU.mult).then_inc(gated_s_done, 1)
                dve.wait_ge(gated_s_done, at(b, 1, 1))
                wait(dve, hT_ps, b, 1, -1)
                nc.vector.tensor_tensor(shared[n][:, :], ps_shared[:, SI:2 * SI], gated_s[:, :],
                                        ALU.mult).then_inc(shared_done, 1)

            def hT(b):
                n = parity(b)
                dve.wait_ge(hT_hi_done, at(b, 1, 1))
                nc.vector.scalar_tensor_tensor(out=hT_lo[n][:, :, :].rearrange("p c s -> p (c s)"),
                                               in0=ps_out[:, 0:3 * S], scalar=0.5,
                                               in1=f32(hT_hi[n][:, :, :]).rearrange("p c s -> p (c s)"),
                                               op0=ALU.mult, op1=ALU.subtract).then_inc(hT_lo_done, 1)

            def output(b):
                n = parity(b)
                dve.wait_ge(out_ps, at(b, 1, 1))
                if isinstance(b, tuple) or b >= 2:
                    dve.wait_ge(out_stored[n], by_parity(shift(b, -2)))
                nc.vector.tensor_tensor(out_sb[n][:, :], ps_out[:, 0:D], row(rows, b),
                                        ALU.add).then_inc(out_done, 1)

            yT(0)
            choose(0)
            weigh(0)

            def step2(b, n):
                if has(n, 1):
                    yT(shift(b, 1))
                gate(b, 0)
                basis(b, 0)
                if has(n, 1):
                    choose(shift(b, 1))
                gate(b, 1)
                basis(b, 1)
                if has(n, -1):
                    hT(shift(b, -1))
                if has(n, 2):
                    moments_of(shift(b, 2), B)
                if has(n, -1):
                    output(shift(b, -1))
                if has(n, 2):
                    normalize(shift(b, 2), B)
                shared_basis(b)
                if has(n, 1):
                    weigh(shift(b, 1))

            steps(dve, step2)
            hT(B - 1)
            output(B - 1)


_INS = ['x', 'ctx_512', 'L0_xattn_Wc', 'L0_xattn_bc', 'L0_ffn_w_router', 'L0_ffn_w_gate', 'L0_ffn_w_up',
        'L0_ffn_w_down', 'L0_ffn_amplitudes', 'L0_ffn_expert_scale', 'L0_ffn_shared_w_gate',
        'L0_ffn_shared_w_up', 'L0_ffn_shared_w_down']
_OUT = ((16, 128, 256), 'float32')


def kernel(**inputs):
    import numpy as _np
    import concourse.bacc as _bacc
    from concourse import mybir as _mybir
    from concourse.bass_utils import run_bass_kernel_spmd as _run

    nc = _bacc.Bacc("TRN2", target_bir_lowering=False, num_devices=1)
    arrays, args = {}, []
    for name in _INS:
        a = _np.ascontiguousarray(inputs[name])
        arrays[f"in_{name}_dram"] = a
        args.append(nc.dram_tensor(f"in_{name}_dram", a.shape, _mybir.dt.from_np(a.dtype), kind="ExternalInput").ap())
    args.append(nc.dram_tensor("out_0_dram", _OUT[0], _mybir.dt.from_np(_np.dtype(_OUT[1])),
                               kind="ExternalOutput").ap())
    build(nc, *args)
    r = _run(nc, [arrays], core_ids=[0])
    return r.results[0]["out_0_dram"]
```

```python
from contextlib import ExitStack

import concourse.bass as bass
from concourse import mybir

F32 = mybir.dt.float32
F32R = mybir.dt.float32r
ALU = mybir.AluOpType
ACT = mybir.ActivationFunctionType
AX = mybir.AxisListType

P = 128
HEADS = 16
GROUPS = 4
PER_GROUP = HEADS // GROUPS
DH = 16
VW = DH + 1
TOPK = 4
LN_EPS = 1e-5
FFN_EPS = 1e-8
SCORE_SCALE = DH ** -0.5
SPARE, TAKEN, BORDER = -3.0e38, -3.3e38, -3.2e38


def build(nc, x, ctx_in, wc, bc, w_router, w_gate, w_up, w_down, amplitudes, expert_scale,
          shared_gate, shared_up, shared_down, out):
    B, S, D = x.shape
    T = ctx_in.shape[1]
    DC = ctx_in.shape[2]
    E = w_router.shape[1]
    K = amplitudes.shape[1]
    I = w_down.shape[0]
    SI = shared_down.shape[0]
    assert (S, T, D, DC, E, I, SI, K) == (P, P, 2 * P, GROUPS * DH, P, P, 2 * P, 8)
    KC = D // P
    HALF_K = K // 2
    UP0, SG0, RT0 = K * I, 2 * K * I, 2 * K * I + 2 * SI
    WCOLS = RT0 + E
    WD0 = KC * WCOLS
    WALL = WD0 + 3 * D
    CONSTS = 1 + 8
    FIRST, LAST = 4, B - 3
    assert (LAST - FIRST + 1) % 2 == 0

    with ExitStack() as stack:
        def sb(name, shape, dt=F32):
            return stack.enter_context(nc.sbuf_tensor(name, shape, dt))

        def sem(name):
            return stack.enter_context(nc.semaphore(name))

        def two(name, shape, dt=F32):
            return [sb(f"{name}{n}", shape, dt) for n in range(2)]

        def f32(ap):
            return ap.bitcast(F32)

        rows = sb("rows", [P, B, D])
        ctx_sb = sb("ctx_sb", [P, B, DC])
        ident_f = sb("ident_f", [P, P])
        ident_r = sb("ident_r", [P, P], F32R)
        zeros_r = sb("zeros_r", [P, 4 * P], F32R)
        neg_half = sb("neg_half", [P, 1])
        wc_sb = sb("wc_sb", [P, 2, D])
        wcT_hi = sb("wcT_hi", [P, 2, D], F32R)
        wcT_lo = sb("wcT_lo", [P, 2, D], F32R)
        bias_bc = sb("bias_bc", [P, D])
        w_all = sb("w_all", [P, WALL])
        w_hi = sb("w_hi", [P, WALL], F32R)
        w_lo = sb("w_lo", [P, WALL], F32R)
        amp = sb("amp", [P, K, 2])
        amp_sq = sb("amp_sq", [P, K, 2])
        power = sb("power", [P, K])
        power_sum = sb("power_sum", [P, 1])
        power_den = sb("power_den", [P, 1])
        power_rec = sb("power_rec", [P, 1])
        escale = sb("escale", [P, 1])
        mix = sb("mix", [P, K])
        neg_sel_f = sb("neg_sel_f", [8, GROUPS, P])
        neg_sel = sb("neg_sel", [8, GROUPS, P], F32R)

        stats = two("stats", [P, 6])
        moments = two("moments", [P, 2])
        var_eps = two("var_eps", [P, 1])
        rstd = two("rstd", [P, 1])
        normed = two("normed", [P, D])
        stats2 = two("stats2", [P, 6])
        moments2 = two("moments2", [P, 2])
        var_eps2 = two("var_eps2", [P, 1])
        rstd2 = two("rstd2", [P, 1])
        normed2 = two("normed2", [P, D])
        x_bias = two("x_bias", [P, D])
        q_parts = two("q_parts", [P, 8, 2, 4 * DH], F32R)
        k_parts = two("k_parts", [P, 2, 2, 4 * DH], F32R)
        v_ones = two("v_ones", [P, GROUPS, VW])
        qT = two("qT", [P, 2, PER_GROUP, S], F32R)
        kT = two("kT", [P, 2, 2, T], F32R)
        row_max = two("row_max", [P, 2, PER_GROUP, 2])
        max_parts = two("max_parts", [P, PER_GROUP, 2, 2, 2], F32R)
        maxT = two("maxT", [8, PER_GROUP, S], F32R)
        probs = [sb(f"probs{u}", [P, PER_GROUP, S]) for u in range(GROUPS)]
        den_rec = two("den_rec", [P, HEADS])
        attn = two("attn", [P, HEADS, DH])
        attnT_hi = two("attnT_hi", [P, KC, S], F32R)
        attnT_lo = two("attnT_lo", [P, KC, S], F32R)

        yT_hi = two("yT_hi", [P, KC, S], F32R)
        yT_lo = two("yT_lo", [P, KC, S], F32R)
        logits = two("logits", [P, E + TOPK])
        top8 = two("top8", [P, 8])
        best4 = two("best4", [P, 8])
        neg_top = two("neg_top", [P, 1])
        replaced = two("replaced", [P, E + TOPK])
        expo = two("expo", [P, E])
        exp_sum = two("exp_sum", [P, 1])
        chosen = two("chosen", [P, E])
        chosen_sum = two("chosen_sum", [P, 1])
        coeff_den = two("coeff_den", [P, 1])
        coeff_rec = two("coeff_rec", [P, 1])
        chosenT = two("chosenT", [P, S])
        coeff = two("coeff", [P, K])
        tanh_g = two("tanh_g", [P, HALF_K * I])
        gated = two("gated", [P, HALF_K * I])
        bases = two("bases", [P, K, I])
        sum4 = sb("sum4", [P, 4, I])
        sum2 = sb("sum2", [P, 2, I])
        zsum = two("zsum", [P, I])
        tanh_s = sb("tanh_s", [P, SI])
        gated_s = sb("gated_s", [P, SI])
        shared = two("shared", [P, SI])
        hT_hi = two("hT_hi", [P, 3, S], F32R)
        hT_lo = two("hT_lo", [P, 3, S], F32R)
        out_sb = two("out_sb", [P, D])

        bank = [stack.enter_context(nc.psum_tensor(f"bank{n}", [P, 512], F32)) for n in range(8)]
        ps_score, ps_gate, ps_up, ps_max = bank[0:2], bank[2], bank[3], bank[4]
        ps_pv, ps_a, ps_b = bank[5], bank[6], bank[7]

        def qT_bank(b, pair):
            return ps_score[1] if isinstance(b, int) and b == 0 and pair == 1 else ps_max

        def max_bank(b, part):
            return (ps_gate, ps_pv, ps_a, ps_max)[part] if isinstance(b, int) and b == 0 else ps_max

        x_loaded = [sem(f"x_loaded{n}") for n in range(2)]
        ctx_loaded = [sem(f"ctx_loaded{n}") for n in range(2)]
        wc_loaded, bias_loaded = sem("wc_loaded"), sem("bias_loaded")
        amp_loaded = sem("amp_loaded")
        w_loaded = [sem(f"w_loaded{n}") for n in range(7)]
        zeroed, ident_made, ident_r_made, zeros_made = (
            sem("zeroed"), sem("ident_made"), sem("ident_r_made"), sem("zeros_made"))
        neg_sel_made, neg_sel_r_made, consts_made = (
            sem("neg_sel_made"), sem("neg_sel_r_made"), sem("consts_made"))
        wcT_ps, wcT_hi_made, wcT_made = sem("wcT_ps"), sem("wcT_hi_made"), sem("wcT_made")
        amp_step = sem("amp_step")
        w_hi_done, w_lo_dve, w_lo_pool = sem("w_hi_done"), sem("w_lo_dve"), sem("w_lo_pool")
        stats_done, moments_done, var_done, rstd_done, normed_done = (
            sem("stats_done"), sem("moments_done"), sem("var_done"), sem("rstd_done"), sem("normed_done"))
        x_bias_done = sem("x_bias_done")
        q_hi_done, q_lo_done, k_hi_done, k_lo_done, v_done = (
            sem("q_hi_done"), sem("q_lo_done"), sem("k_hi_done"), sem("k_lo_done"), sem("v_done"))
        stats2_done, moments2_done, var2_done, rstd2_done, normed2_done = (
            sem("stats2_done"), sem("moments2_done"), sem("var2_done"), sem("rstd2_done"), sem("normed2_done"))
        qT_ps, qT_done = sem("qT_ps"), sem("qT_done")
        kT_ps, kT_done = sem("kT_ps"), sem("kT_done")
        max_ps, max_done = sem("max_ps"), sem("max_done")
        max_hi_done, max_lo_done, maxT_ps, maxT_done = (
            sem("max_hi_done"), sem("max_lo_done"), sem("maxT_ps"), sem("maxT_done"))
        score_ps, probs_done, pv_ps = sem("score_ps"), sem("probs_done"), sem("pv_ps")
        den_rec_done, attn_done, attnT_ps, attnT_hi_done, attnT_lo_done, proj_ps, x1_done = (
            sem("den_rec_done"), sem("attn_done"), sem("attnT_ps"), sem("attnT_hi_done"),
            sem("attnT_lo_done"), sem("proj_ps"), sem("x1_done"))

        yT_ps, yT_hi_done, yT_lo_done = sem("yT_ps"), sem("yT_hi_done"), sem("yT_lo_done")
        route_ps, logits_done, top8_done, neg_top_done, best4_done = (
            sem("route_ps"), sem("logits_done"), sem("top8_done"), sem("neg_top_done"), sem("best4_done"))
        exp_done, replaced_done, chosen_done, coeff_den_done, coeff_rec_done = (
            sem("exp_done"), sem("replaced_done"), sem("chosen_done"), sem("coeff_den_done"),
            sem("coeff_rec_done"))
        chosenT_ps, chosenT_done, coeff_ps, coeff_done = (
            sem("chosenT_ps"), sem("chosenT_done"), sem("coeff_ps"), sem("coeff_done"))
        gate_ps, up_ps, tanh_done, gated_done, bases_done = (
            sem("gate_ps"), sem("up_ps"), sem("tanh_done"), sem("gated_done"), sem("bases_done"))
        sum_step, z_done = sem("sum_step"), sem("z_done")
        shared_ps, tanh_s_done, gated_s_done, shared_done = (
            sem("shared_ps"), sem("tanh_s_done"), sem("gated_s_done"), sem("shared_done"))
        hT_ps, hT_hi_done, hT_lo_done, out_ps, out_done = (
            sem("hT_ps"), sem("hT_hi_done"), sem("hT_lo_done"), sem("out_ps"), sem("out_done"))
        out_stored = [sem(f"out_stored{n}") for n in range(2)]

        block = stack.enter_context(nc.Block())

        def parity(b):
            return (FIRST + b[1]) % 2 if isinstance(b, tuple) else b % 2

        def at(b, per=1, plus=0):
            if isinstance(b, tuple):
                return b[0] * (2 * per) + (per * (FIRST + b[1]) + plus)
            return per * b + plus

        def by_parity(b):
            if isinstance(b, tuple):
                return b[0] * 16 + 16 * ((FIRST + b[1]) // 2 + 1)
            return 16 * (b // 2 + 1)

        def shift(b, by):
            return (b[0], b[1] + by) if isinstance(b, tuple) else b + by

        def row(t, b):
            if isinstance(b, tuple):
                return t[:, bass.ds(b[0] * 2 + (FIRST + b[1]), 1), :].rearrange("p a d -> p (a d)")
            return t[:, b, :]

        def keys_twice(b, a):
            c = row(ctx_sb, b)[:, 2 * DH * a:2 * DH * (a + 1)]
            return c.rearrange("p (r u d) -> p r u d", r=2, u=1).to_broadcast([P, 2, 2, DH])

        def heads_of(t):
            return t[:, :].rearrange("p (a t d) -> p a t d", a=2, d=DH)

        def q_place(n, part):
            return q_parts[n][:, :, :, part * DH:(part + 1) * DH].rearrange("p t a d -> p a t d")

        def group_of(u):
            return 2 * (u % 2) + u // 2

        def run(eng, step):
            for b in range(FIRST):
                step(b, b)
            with eng.Fori(0, (LAST - FIRST + 1) // 2) as r:
                for n in range(2):
                    step((r, n), None)
            for b in range(LAST + 1, B + 3):
                step(b, b)

        def has(n, by):
            return n is None or 0 <= n + by < B

        def wait(eng, s, b, per=1, plus=0, n=0):
            v = at(b, per, plus)
            if isinstance(b, tuple) or v > 0:
                eng.wait_ge(s, v)

        def wait_alone(eng, s, v):
            if not isinstance(v, int):
                v = eng.to_reg(v)
            eng.wait_ge(consts_made, CONSTS)
            if not isinstance(v, int) or v > 0:
                eng.wait_ge(s, v)

        w_view = w_all[:, 0:WD0].rearrange("p (c n) -> p c n", c=KC)
        w_hi_view = w_hi[:, 0:WD0].rearrange("p (c n) -> p c n", c=KC)
        w_lo_view = w_lo[:, 0:WD0].rearrange("p (c n) -> p c n", c=KC)

        def w_piece(n, t, view):
            c0, width = ((RT0, E), (0, K * I), (UP0, K * I), (SG0, SI), (SG0 + SI, SI))[n] if n < 5 else (0, 0)
            if n < 5:
                return view[:, :, c0:c0 + width]
            if n == 5:
                return t[:, WD0:WD0 + D].rearrange("p (c n) -> p c n", c=1)
            return t[:, WD0 + D:WALL].rearrange("p (c n) -> p c n", c=2)

        w_sources = [w_router, w_gate, w_up, shared_gate, shared_up, w_down, shared_down]
        WARM = dict(start=14, qT=6, max=6, maxT=3, a=3, b=3, c=3, d=3, e=4)
        ON_POOL = (1, 2)

        @block.sync
        def _(sp):
            def load(b):
                n = parity(b)
                sp.dma_start(row(rows, b), dram_row(x, b)).then_inc(x_loaded[n], 16)
                sp.dma_start(row(ctx_sb, b), dram_row(ctx_in, b)).then_inc(ctx_loaded[n], 16)

            def dram_row(t, b):
                if isinstance(b, tuple):
                    return t[bass.ds(b[0] * 2 + (FIRST + b[1]), 1), :, :].rearrange("a p d -> (a p) d")
                return t[b]

            def load_weights(n):
                src = w_sources[n]
                sp.dma_start(w_piece(n, w_all, w_view),
                             src.rearrange("(c p) n -> p c n", p=P)).then_inc(w_loaded[n], 16)

            def load_next(b):
                before = shift(b, -2)
                sp.wait_ge(x_loaded[parity(b)], by_parity(before))
                sp.wait_ge(ctx_loaded[parity(b)], by_parity(before))
                load(b)

            for b in range(2):
                load(b)
            sp.dma_start(wc_sb[:, :, :], wc.rearrange("(m p) d -> p m d", p=P)).then_inc(wc_loaded, 16)
            for n in range(3):
                load_weights(n)
            for b in range(2, 4):
                load_next(b)
            for n in range(3, 7):
                load_weights(n)
            for b in range(4, FIRST + 2):
                load_next(b)
            with sp.Fori(0, (LAST - FIRST + 1) // 2) as r:
                for n in range(2):
                    load_next((r, n + 2))

            def store(b, n):
                sp.wait_ge(out_done, at(b, 1, 1))
                if isinstance(b, tuple):
                    dst = out[bass.ds(b[0] * 2 + (FIRST + b[1]), 1), :, :].rearrange("a p d -> (a p) d")
                else:
                    dst = out[b]
                sp.dma_start(dst, out_sb[parity(b)][:, :]).then_inc(out_stored[parity(b)], 16)

            for b in range(FIRST):
                store(b, b)
            with sp.Fori(0, (LAST - FIRST + 1) // 2) as r:
                for n in range(2):
                    store((r, n), None)
            for b in range(LAST + 1, B):
                store(b, b)
            for n in range(2):
                sp.wait_ge(out_stored[n], 16 * (B // 2))

        @block.gpsimd
        def _(pool):
            nc.gpsimd.memset(ident_f[:, :], 0.0).then_inc(zeroed, 1)
            pool.wait_ge(zeroed, 1)
            nc.gpsimd.affine_select(out=ident_f[:, :], in_=ident_f[:, :], compare_op=ALU.not_equal,
                                    fill=1.0, base=0, pattern=[[-1, P]],
                                    channel_multiplier=1).then_inc(ident_made, 1)
            nc.gpsimd.memset(neg_half[:, :], -0.5).then_inc(consts_made, 1)
            nc.gpsimd.memset(neg_sel_f[:, :, :], 0.0).then_inc(zeroed, 1)
            pool.wait_ge(zeroed, 2)
            for part in range(2):
                nc.gpsimd.affine_select(out=neg_sel_f[:, :, :], in_=neg_sel_f[:, :, :],
                                        compare_op=ALU.not_equal, fill=-1.0, base=-part,
                                        pattern=[[-2, GROUPS], [0, P]],
                                        channel_multiplier=1).then_inc(neg_sel_made, 1)
                pool.wait_ge(neg_sel_made, 1 + part)
            def rsqrt(b):
                n = parity(b)
                pool.wait_ge(var_done, at(b, 1, 1))
                nc.gpsimd.tensor_tensor(rstd[n][:, :], var_eps[n][:, :], neg_half[:, :],
                                        ALU.pow).then_inc(rstd_done, 1)

            def rsqrt2(b):
                n = parity(b)
                pool.wait_ge(var2_done, at(b, 1, 1))
                nc.gpsimd.tensor_tensor(rstd2[n][:, :], var_eps2[n][:, :], neg_half[:, :],
                                        ALU.pow).then_inc(rstd2_done, 1)

            def add_bias(b):
                n = parity(b)
                pool.wait_ge(x_loaded[n], by_parity(b))
                wait(pool, x1_done, b, 1, -1)
                nc.gpsimd.tensor_tensor(x_bias[n][:, :], row(rows, b), bias_bc[:, :],
                                        ALU.add).then_inc(x_bias_done, 1)

            def weights_lo(n):
                pool.wait_ge(w_hi_done, n + 1)
                nc.gpsimd.tensor_tensor(w_piece(n, w_lo, w_lo_view), w_piece(n, w_all, w_view),
                                        f32(w_piece(n, w_hi, w_hi_view)), ALU.subtract).then_inc(w_lo_pool, 1)

            def sum_bases(b):
                n = parity(b)
                pool.wait_ge(bases_done, at(b, 2, 2))
                nc.gpsimd.tensor_tensor(sum4[:, :, :], bases[n][:, 0:4, :], bases[n][:, 4:8, :],
                                        ALU.add).then_inc(sum_step, 1)
                pool.wait_ge(sum_step, at(b, 2, 1))
                nc.gpsimd.tensor_tensor(sum2[:, :, :], sum4[:, 0:2, :], sum4[:, 2:4, :],
                                        ALU.add).then_inc(sum_step, 1)
                pool.wait_ge(sum_step, at(b, 2, 2))
                nc.gpsimd.tensor_tensor(zsum[n][:, :], sum2[:, 0, :], sum2[:, 1, :],
                                        ALU.add).then_inc(z_done, 1)

            rsqrt(0)
            rsqrt(1)
            weights_lo(ON_POOL[0])
            pool.wait_ge(bias_loaded, 16)

            def step(b, n):
                if has(n, -1):
                    rsqrt2(shift(b, -1))
                if has(n, 2):
                    rsqrt(shift(b, 2))
                if has(n, 0):
                    add_bias(b)
                if n == 0:
                    weights_lo(ON_POOL[1])
                if has(n, -2):
                    sum_bases(shift(b, -2))

            run(pool, step)

        @block.scalar
        def _(act):
            act.dma_start(bias_bc[:, :], bc.partition_broadcast(P)).then_inc(bias_loaded, 16)
            act.dma_start(amp[:, :, :], amplitudes).then_inc(amp_loaded, 16)
            act.dma_start(escale[:, :], expert_scale.rearrange("(e a) -> e a", a=1)).then_inc(amp_loaded, 16)

            def keys(b):
                n = parity(b)
                act.wait_ge(ctx_loaded[n], by_parity(b))
                wait_alone(act, kT_ps, at(b, 1, -1))
                for a in range(2):
                    t = nc.scalar.activation(
                        k_parts[n][:, :, a, 0:2 * DH].rearrange("p r (u d) -> p r u d", u=2),
                        keys_twice(b, a), ACT.Copy)
                t.then_inc(k_hi_done, 1)

            def values(b):
                n = parity(b)
                wait_alone(act, pv_ps, at(b, 4, -4))
                nc.scalar.activation(v_ones[n][:, :, 0:DH], row(ctx_sb, b).rearrange("p (g d) -> p g d", g=GROUPS),
                                     ACT.Copy).then_inc(v_done, 1)

            def q_hi(b):
                n = parity(b)
                act.wait_ge(normed_done, at(b, 1, 1))
                wait(act, qT_ps, b, 2, -2)
                for u in range(2):
                    t = nc.scalar.activation(q_place(n, 2 * u), heads_of(normed[n]), ACT.Copy)
                t.then_inc(q_hi_done, 1)

            def evacuate_qT(b, pair):
                n = parity(b)
                act.wait_ge(qT_ps, at(b, 2, pair + 1))
                nc.scalar.activation(qT[n][:, pair, :, :].rearrange("p j s -> p (j s)"), qT_bank(b, pair)[:, :],
                                     ACT.Copy).then_inc(qT_done, 1)

            def evacuate_kT(b):
                n = parity(b)
                act.wait_ge(kT_ps, at(b, 1, 1))
                src = ps_b[:, 0:2 * T].rearrange("p (a t) -> p a t", a=2)
                nc.scalar.activation(kT[n][0:64, :, 0, :], src[0:64, :, :], ACT.Copy)
                nc.scalar.activation(kT[n][64:128, :, 1, :], src[64:128, :, :], ACT.Copy).then_inc(kT_done, 1)

            def evacuate_maxT(b):
                n = parity(b)
                act.wait_ge(maxT_ps, at(b, 1, 1))
                nc.scalar.activation(maxT[n][:, :, :].rearrange("p j s -> p (j s)"),
                                     ps_b[0:8, :], ACT.Copy).then_inc(maxT_done, 1)

            def exps(b, u):
                act.wait_ge(score_ps, at(b, 4, u + 1))
                nc.scalar.activation(probs[u][:, :, :].rearrange("p j s -> p (j s)"), ps_score[u % 2][:, :],
                                     ACT.Exp, scale=SCORE_SCALE).then_inc(probs_done, 1)

            def attnT(b):
                n = parity(b)
                act.wait_ge(attnT_ps, at(b, 1, 1))
                nc.scalar.activation(attnT_hi[n][:, :, :].rearrange("p c s -> p (c s)"),
                                     ps_a[:, 0:KC * S], ACT.Copy).then_inc(attnT_hi_done, 1)

            def weight_hi(n):
                act.wait_ge(w_loaded[n], 16)
                nc.scalar.activation(w_piece(n, w_hi, w_hi_view), w_piece(n, w_all, w_view),
                                     ACT.Copy).then_inc(w_hi_done, 1)

            act.wait_ge(ident_made, 1)
            nc.scalar.activation(ident_r[:, :], ident_f[:, :], ACT.Copy).then_inc(ident_r_made, 1)
            keys(0)
            q_hi(0)
            evacuate_qT(0, 0)
            evacuate_kT(0)
            evacuate_qT(0, 1)
            act.wait_ge(wcT_ps, 1)
            nc.scalar.activation(wcT_hi[:, :, :].rearrange("p c n -> p (c n)"), ps_score[0][:, :],
                                 ACT.Copy).then_inc(wcT_hi_made, 1)
            keys(1)
            q_hi(1)
            values(0)
            for n in (0, 1):
                weight_hi(n)
            evacuate_maxT(0)

            def yT(b):
                n = parity(b)
                act.wait_ge(yT_ps, at(b, 1, 1))
                nc.scalar.activation(yT_hi[n][:, :, :].rearrange("p c s -> p (c s)"),
                                     ps_a[:, 0:KC * S], ACT.Copy).then_inc(yT_hi_done, 1)

            def copy_logits(b):
                n = parity(b)
                act.wait_ge(route_ps, at(b, 1, 1))
                nc.scalar.activation(logits[n][:, 0:E], ps_a[:, 0:E], ACT.Copy).then_inc(logits_done, 1)

            def exp_logits(b):
                n = parity(b)
                act.wait_ge(neg_top_done, at(b, 1, 1))
                nc.scalar.activation(expo[n][:, :], logits[n][:, 0:E], ACT.Exp, bias=neg_top[n][:, 0:1],
                                     accum_out=exp_sum[n][:, 0:1]).then_inc(exp_done, 1)

            def copy_chosenT(b):
                n = parity(b)
                act.wait_ge(chosenT_ps, at(b, 1, 1))
                nc.scalar.activation(chosenT[n][:, :], ps_a[:, E:E + S], ACT.Copy).then_inc(chosenT_done, 1)

            def tanh(b, half):
                act.wait_ge(gate_ps, at(b, 2, half + 1))
                nc.scalar.activation(tanh_g[half][:, :], ps_gate[:, :], ACT.Tanh,
                                     scale=0.5).then_inc(tanh_done, 1)

            def tanh_shared(b):
                act.wait_ge(shared_ps, at(b, 1, 1))
                nc.scalar.activation(tanh_s[:, :], ps_gate[:, 0:SI], ACT.Tanh,
                                     scale=0.5).then_inc(tanh_s_done, 1)

            def hT(b):
                n = parity(b)
                act.wait_ge(hT_ps, at(b, 1, 1))
                nc.scalar.activation(hT_hi[n][:, :, :].rearrange("p c s -> p (c s)"), ps_b[:, 0:3 * S],
                                     ACT.Copy, scale=0.5).then_inc(hT_hi_done, 1)

            def step(b, n):
                e, f, g = shift(b, -1), shift(b, -2), shift(b, -3)
                now, route, ffn, end = has(n, 0), has(n, -1), has(n, -2), has(n, -3)
                ahead, ahead2 = has(n, 1), has(n, 2)
                if ahead:
                    evacuate_qT(shift(b, 1), 0)
                if now:
                    exps(b, 0)
                    exps(b, 1)
                if ahead:
                    evacuate_kT(shift(b, 1))
                if n == 1:
                    for piece in range(3, 7):
                        weight_hi(piece)
                if ffn:
                    tanh(f, 0)
                if ahead2:
                    keys(shift(b, 2))
                    q_hi(shift(b, 2))
                if now:
                    exps(b, 2)
                if ahead:
                    evacuate_qT(shift(b, 1), 1)
                if route:
                    yT(e)
                if now:
                    exps(b, 3)
                if n == 0:
                    weight_hi(2)
                if ahead:
                    values(shift(b, 1))
                if end:
                    hT(g)
                if route:
                    copy_logits(e)
                if ffn:
                    tanh(f, 1)
                if route:
                    exp_logits(e)
                    copy_chosenT(e)
                if now:
                    attnT(b)
                if ffn:
                    tanh_shared(f)
                if ahead:
                    evacuate_maxT(shift(b, 1))

            run(act, step)

        @block.tensor
        def _(pe):
            def transpose_q(b, pair):
                n = parity(b)
                if pair == 0:
                    pe.wait_ge(q_lo_done, at(b, 1, 1))
                elif isinstance(b, tuple) or b > 0:
                    pe.wait_ge(qT_done, at(b, 2, 1))
                for j in range(PER_GROUP):
                    src = q_parts[n][:, PER_GROUP * pair + j, :, :].rearrange("p a d -> p (a d)")
                    t = nc.tensor.transpose(qT_bank(b, pair)[:, j * S:(j + 1) * S].bitcast(F32R), src, ident_r[:, :])
                t.then_inc(qT_ps, 1)

            def transpose_k(b):
                n = parity(b)
                pe.wait_ge(k_lo_done, at(b, 1, 1))
                for pair in range(2):
                    t = nc.tensor.transpose(ps_b[:, pair * T:(pair + 1) * T].bitcast(F32R),
                                            k_parts[n][:, pair, :, :].rearrange("p a d -> p (a d)"),
                                            ident_r[:, :])
                t.then_inc(kT_ps, 1)

            def max_scores(b, part):
                n, pair = parity(b), part // 2
                if part == 0:
                    pe.wait_ge(qT_done, at(b, 2, 2))
                elif isinstance(b, tuple) or b > 0:
                    pe.wait_ge(max_done, at(b, 4, part))
                for u in range(2):
                    t = nc.tensor.matmul(max_bank(b, part)[:, 2 * T * u:2 * T * (u + 1)],
                                         qT[n][:, pair, 2 * (part % 2) + u, :],
                                         kT[n][:, pair, :, :].rearrange("p a t -> p (a t)"),
                                         start=True, stop=True)
                t.then_inc(max_ps, 1)

            def transpose_max(b):
                n = parity(b)
                pe.wait_ge(max_lo_done, at(b, 1, 1))
                if isinstance(b, tuple) or b >= 4:
                    pe.wait_ge(out_done, at(b, 1, -3))
                for j in range(PER_GROUP):
                    t = nc.tensor.transpose(ps_b[0:8, j * S:(j + 1) * S].bitcast(F32R),
                                            max_parts[n][:, j, :, :, :].rearrange("p a b c -> p (a b c)"),
                                            ident_r[:, :])
                t.then_inc(maxT_ps, 1)

            def scores(b, u):
                n, pair, a = parity(b), u // 2, u % 2
                if u == 0:
                    pe.wait_ge(maxT_done, at(b, 1, 1))
                if u >= 2:
                    pe.wait_ge(probs_done, at(b, 4, u - 1))
                nc.tensor.matmul(ps_score[u % 2][:, :], kT[n][64 * a:64 * a + 64, pair, a, :],
                                 qT[n][64 * a:64 * a + 64, pair, :, :].rearrange("p j s -> p (j s)"),
                                 start=True, stop=False)
                nc.tensor.matmul(ps_score[u % 2][:, :], neg_sel[:, u, :],
                                 maxT[n][:, :, :].rearrange("p j s -> p (j s)"),
                                 start=False, stop=True).then_inc(score_ps, 1)

            def values(b, u):
                pe.wait_ge(probs_done, at(b, 4, u + 1))
                g = group_of(u)
                if u == 0:
                    pe.wait_ge(v_done, at(b, 1, 1))
                    wait(pe, attn_done, b)
                for j in range(PER_GROUP):
                    h = PER_GROUP * g + j
                    t = nc.tensor.matmul(ps_pv[:, h * VW:(h + 1) * VW], probs[u][:, j, :],
                                         v_ones[parity(b)][:, g, :], start=True, stop=True)
                t.then_inc(pv_ps, 1)

            def transpose_attn(b):
                n = parity(b)
                pe.wait_ge(attn_done, at(b, 1, 1))
                wait(pe, coeff_done, b)
                for c in range(KC):
                    t = nc.tensor.transpose(ps_a[:, c * S:(c + 1) * S],
                                            attn[n][:, 8 * c:8 * c + 8, :].rearrange("p h d -> p (h d)"),
                                            ident_f[:, :])
                t.then_inc(attnT_ps, 1)

            def three_passes(dst, hi, lo, rhs_hi, rhs_lo, chunks):
                k = 0
                for c in range(chunks):
                    for l, r in ((hi, rhs_hi), (hi, rhs_lo), (lo, rhs_hi)):
                        t = nc.tensor.matmul(dst, l(c), r(c), start=(k == 0), stop=(k == 3 * chunks - 1))
                        k += 1
                return t

            def project(b):
                n = parity(b)
                pe.wait_ge(attnT_lo_done, at(b, 1, 1))
                three_passes(ps_a[:, 0:D], lambda c: attnT_hi[n][:, c, :], lambda c: attnT_lo[n][:, c, :],
                             lambda c: wcT_hi[:, c, :], lambda c: wcT_lo[:, c, :], KC).then_inc(proj_ps, 1)

            def keep_warm(count):
                for _ in range(count):
                    nc.tensor.matmul(ps_up[:, :], zeros_r[:, 0:P], zeros_r[:, :], start=True, stop=True)

            pe.wait_ge(zeros_made, 1)
            keep_warm(WARM["start"])
            pe.wait_ge(ident_r_made, 1)
            transpose_q(0, 0)
            transpose_k(0)
            transpose_q(0, 1)
            pe.wait_ge(wc_loaded, 16)
            for c in range(KC):
                for m in range(2):
                    t = nc.tensor.transpose(ps_score[0][:, c * D + m * P:c * D + (m + 1) * P],
                                            wc_sb[:, m, c * P:(c + 1) * P], ident_f[:, :])
            t.then_inc(wcT_ps, 1)
            keep_warm(WARM["qT"])
            for part in range(4):
                max_scores(0, part)
            keep_warm(WARM["max"])
            transpose_max(0)
            keep_warm(WARM["maxT"])
            pe.wait_ge(wcT_made, 1)
            pe.wait_ge(neg_sel_r_made, 1)

            def transpose_y(b):
                n = parity(b)
                pe.wait_ge(normed2_done, at(b, 1, 1))
                for c in range(KC):
                    t = nc.tensor.transpose(ps_a[:, c * S:(c + 1) * S], normed2[n][:, c * P:(c + 1) * P],
                                            ident_f[:, :])
                t.then_inc(yT_ps, 1)

            def weights(b, dst, c0, width):
                n = parity(b)
                return three_passes(dst, lambda c: yT_hi[n][:, c, :], lambda c: yT_lo[n][:, c, :],
                                    lambda c: w_hi[:, c * WCOLS + c0:c * WCOLS + c0 + width],
                                    lambda c: w_lo[:, c * WCOLS + c0:c * WCOLS + c0 + width], KC)

            def route(b):
                pe.wait_ge(yT_lo_done, at(b, 1, 1))
                weights(b, ps_a[:, 0:E], RT0, E).then_inc(route_ps, 1)

            def transpose_chosen(b):
                pe.wait_ge(chosen_done, at(b, 1, 1))
                nc.tensor.transpose(ps_a[:, E:E + S], chosen[parity(b)][:, :],
                                    ident_f[:, :]).then_inc(chosenT_ps, 1)

            def mix_experts(b):
                pe.wait_ge(chosenT_done, at(b, 1, 1))
                nc.tensor.matmul(ps_a[:, E + S:E + S + K], chosenT[parity(b)][:, :], mix[:, :],
                                 start=True, stop=True).then_inc(coeff_ps, 1)

            def gate(b, half):
                if half == 0:
                    wait(pe, shared_done, b)
                else:
                    pe.wait_ge(gated_done, at(b, 2, 1))
                weights(b, ps_gate[:, :], half * HALF_K * I, HALF_K * I).then_inc(gate_ps, 1)

            def up(b, half):
                wait(pe, bases_done, b, 2, half)
                weights(b, ps_up[:, :], UP0 + half * HALF_K * I, HALF_K * I).then_inc(up_ps, 1)

            def shared_in(b):
                pe.wait_ge(gated_done, at(b, 2, 2))
                weights(b, ps_gate[:, :], SG0, 2 * SI).then_inc(shared_ps, 1)

            def transpose_h(b):
                n = parity(b)
                pe.wait_ge(z_done, at(b, 1, 1))
                pe.wait_ge(shared_done, at(b, 1, 1))
                if isinstance(b, tuple) or b + 4 < B:
                    pe.wait_ge(kT_done, at(b, 1, 5))
                elif b + 3 >= B:
                    pe.wait_ge(out_done, b)
                nc.tensor.transpose(ps_b[:, 0:S], zsum[n][:, :], ident_f[:, :])
                for c in range(2):
                    t = nc.tensor.transpose(ps_b[:, (c + 1) * S:(c + 2) * S], shared[n][:, c * P:(c + 1) * P],
                                            ident_f[:, :])
                t.then_inc(hT_ps, 1)

            def down(b):
                n = parity(b)
                pe.wait_ge(hT_lo_done, at(b, 1, 1))
                three_passes(ps_b[:, 0:D], lambda c: hT_hi[n][:, c, :], lambda c: hT_lo[n][:, c, :],
                             lambda c: w_hi[:, WD0 + c * D:WD0 + (c + 1) * D],
                             lambda c: w_lo[:, WD0 + c * D:WD0 + (c + 1) * D], 3).then_inc(out_ps, 1)

            def step(b, n):
                e, f, g = shift(b, -1), shift(b, -2), shift(b, -3)
                now, router, ffn, end, ahead = has(n, 0), has(n, -1), has(n, -2), has(n, -3), has(n, 1)
                if ahead:
                    transpose_q(shift(b, 1), 0)
                if now:
                    scores(b, 0)
                    scores(b, 1)
                if ahead:
                    transpose_k(shift(b, 1))
                if n == 2:
                    pe.wait_ge(w_lo_dve, 7 - len(ON_POOL))
                    pe.wait_ge(w_lo_pool, len(ON_POOL))
                if ffn:
                    gate(f, 0)
                elif n is not None and n < 2:
                    keep_warm(WARM["a"])
                if now:
                    values(b, 0)
                    scores(b, 2)
                if ahead:
                    transpose_q(shift(b, 1), 1)
                if router:
                    transpose_y(e)
                if ffn:
                    up(f, 0)
                elif n is not None and n < 2:
                    keep_warm(WARM["b"])
                if now:
                    values(b, 1)
                    scores(b, 3)
                if end:
                    transpose_h(g)
                if n == 1:
                    pe.wait_ge(w_lo_dve, 1)
                    pe.wait_ge(amp_step, 6)
                if router:
                    route(e)
                if ahead:
                    max_scores(shift(b, 1), 0)
                if ffn:
                    gate(f, 1)
                elif n is not None and n < 2:
                    keep_warm(WARM["c"])
                if now:
                    values(b, 2)
                if ahead:
                    max_scores(shift(b, 1), 1)
                if ffn:
                    up(f, 1)
                elif n is not None and n < 2:
                    keep_warm(WARM["d"])
                if now:
                    values(b, 3)
                if ahead:
                    max_scores(shift(b, 1), 2)
                if router:
                    transpose_chosen(e)
                if end:
                    down(g)
                if router:
                    mix_experts(e)
                if ahead:
                    max_scores(shift(b, 1), 3)
                if now:
                    transpose_attn(b)
                if ffn:
                    shared_in(f)
                elif n is not None and n < 2:
                    keep_warm(WARM["e"])
                if ahead:
                    transpose_max(shift(b, 1))
                if now:
                    project(b)

            run(pe, step)

        @block.vector
        def _(dve):
            def moments_of(b):
                n = parity(b)
                dve.wait_ge(x_loaded[n], by_parity(b))
                nc.vector.bn_stats(stats[n][:, :], row(rows, b)).then_inc(stats_done, 1)
                wait_alone(dve, stats_done, at(b, 1, 1))
                nc.vector.bn_aggr(moments[n][:, :], stats[n][:, :]).then_inc(moments_done, 1)
                dve.wait_ge(moments_done, at(b, 1, 1))
                nc.vector.tensor_scalar(var_eps[n][:, :], moments[n][:, 1:2], LN_EPS, None,
                                        ALU.add).then_inc(var_done, 1)

            def normalize(b):
                n = parity(b)
                dve.wait_ge(rstd_done, at(b, 1, 1))
                nc.vector.tensor_scalar(normed[n][:, :], row(rows, b), moments[n][:, 0:1], rstd[n][:, 0:1],
                                        ALU.subtract, ALU.mult).then_inc(normed_done, 1)

            def moments2_of(b):
                n = parity(b)
                wait_alone(dve, x1_done, at(b, 1, 1))
                nc.vector.bn_stats(stats2[n][:, :], row(rows, b)).then_inc(stats2_done, 1)
                wait_alone(dve, stats2_done, at(b, 1, 1))
                nc.vector.bn_aggr(moments2[n][:, :], stats2[n][:, :]).then_inc(moments2_done, 1)
                dve.wait_ge(moments2_done, at(b, 1, 1))
                nc.vector.tensor_scalar(var_eps2[n][:, :], moments2[n][:, 1:2], LN_EPS, None,
                                        ALU.add).then_inc(var2_done, 1)

            def normalize2(b):
                n = parity(b)
                dve.wait_ge(rstd2_done, at(b, 1, 1))
                nc.vector.tensor_scalar(normed2[n][:, :], row(rows, b), moments2[n][:, 0:1], rstd2[n][:, 0:1],
                                        ALU.subtract, ALU.mult).then_inc(normed2_done, 1)

            def k_lo(b):
                n = parity(b)
                dve.wait_ge(k_hi_done, at(b, 1, 1))
                for a in range(2):
                    hi, lo = (k_parts[n][:, :, a, c:c + 2 * DH].rearrange("p r (u d) -> p r u d", u=2)
                              for c in (0, 2 * DH))
                    t = nc.vector.tensor_tensor(lo, keys_twice(b, a), f32(hi), ALU.subtract)
                t.then_inc(k_lo_done, 1)

            def q_lo(b):
                n = parity(b)
                dve.wait_ge(q_hi_done, at(b, 1, 1))
                for u in range(2):
                    t = nc.vector.tensor_tensor(q_place(n, 2 * u + 1), heads_of(normed[n]),
                                                f32(q_place(n, 2 * u)), ALU.subtract)
                t.then_inc(q_lo_done, 1)

            def maxima(b, part):
                n = parity(b)
                dve.wait_ge(max_ps, at(b, 4, part + 1))
                dst = row_max[n][:, part // 2, 2 * (part % 2):2 * (part % 2) + 2, :].rearrange("p j a -> p (j a)")
                nc.vector.tensor_reduce(dst, max_bank(b, part)[:, :].rearrange("p (x t) -> p x t", t=T),
                                        AX.X, ALU.max).then_inc(max_done, 1)

            def split_max(b):
                n = parity(b)
                dve.wait_ge(max_done, at(b, 4, 4))
                view = max_parts[n][:, :, :, :, :].rearrange("p j r a c -> p r j a c")
                nc.vector.tensor_copy(view[:, :, :, :, 0], row_max[n][:, :, :, :]).then_inc(max_hi_done, 1)
                dve.wait_ge(max_hi_done, at(b, 1, 1))
                nc.vector.tensor_tensor(view[:, :, :, :, 1], row_max[n][:, :, :, :], f32(view[:, :, :, :, 0]),
                                        ALU.subtract).then_inc(max_lo_done, 1)

            def divide(b):
                n = parity(b)
                dve.wait_ge(pv_ps, at(b, 4, 4))
                pv = ps_pv[:, 0:HEADS * VW].rearrange("p (h w) -> p h w", w=VW)
                nc.vector.reciprocal(den_rec[n][:, :], pv[:, :, DH]).then_inc(den_rec_done, 1)
                dve.wait_ge(den_rec_done, at(b, 1, 1))
                nc.vector.tensor_tensor(
                    attn[n][:, :, :], pv[:, :, 0:DH],
                    den_rec[n][:, :].rearrange("p (h a) -> p h a", a=1).to_broadcast([P, HEADS, DH]),
                    ALU.mult).then_inc(attn_done, 1)

            def attnT(b):
                n = parity(b)
                dve.wait_ge(attnT_hi_done, at(b, 1, 1))
                nc.vector.tensor_tensor(attnT_lo[n][:, :, :].rearrange("p c s -> p (c s)"), ps_a[:, 0:KC * S],
                                        f32(attnT_hi[n][:, :, :]).rearrange("p c s -> p (c s)"),
                                        ALU.subtract).then_inc(attnT_lo_done, 1)

            def residual(b):
                n = parity(b)
                dve.wait_ge(proj_ps, at(b, 1, 1))
                dve.wait_ge(x_bias_done, at(b, 1, 1))
                nc.vector.tensor_tensor(row(rows, b), ps_a[:, 0:D], x_bias[n][:, :],
                                        ALU.add).then_inc(x1_done, 1)

            nc.vector.memset(f32(zeros_r[:, :]), 0.0).then_inc(zeros_made, 1)
            for n in range(2):
                nc.vector.memset(f32(kT[n][:, :, :, :]), 0.0).then_inc(consts_made, 1)
                nc.vector.memset(v_ones[n][:, :, DH:VW], 1.0).then_inc(consts_made, 1)
                nc.vector.memset(logits[n][:, E:E + TOPK], SPARE).then_inc(consts_made, 1)
                nc.vector.memset(best4[n][:, TOPK:8], SPARE).then_inc(consts_made, 1)
            moments_of(0)
            normalize(0)
            k_lo(0)
            q_lo(0)
            moments_of(1)
            normalize(1)
            dve.wait_ge(neg_sel_made, 2)
            nc.vector.tensor_copy(neg_sel[:, :, :], neg_sel_f[:, :, :]).then_inc(neg_sel_r_made, 1)
            for part in range(4):
                maxima(0, part)
            split_max(0)
            dve.wait_ge(wcT_hi_made, 1)
            nc.vector.tensor_tensor(wcT_lo[:, :, :].rearrange("p c n -> p (c n)"), ps_score[0][:, :],
                                    f32(wcT_hi[:, :, :]).rearrange("p c n -> p (c n)"),
                                    ALU.subtract).then_inc(wcT_made, 1)
            k_lo(1)
            q_lo(1)

            def weight_lo(n):
                dve.wait_ge(w_hi_done, n + 1)
                nc.vector.tensor_tensor(w_piece(n, w_lo, w_lo_view), w_piece(n, w_all, w_view),
                                        f32(w_piece(n, w_hi, w_hi_view)), ALU.subtract).then_inc(w_lo_dve, 1)

            weight_lo(0)

            dve.wait_ge(amp_loaded, 32)
            nc.vector.tensor_tensor(amp_sq[:, :, :], amp[:, :, :], amp[:, :, :], ALU.mult).then_inc(amp_step, 1)
            dve.wait_ge(amp_step, 1)
            nc.vector.tensor_reduce(power[:, :], amp_sq[:, :, :], AX.X, ALU.add).then_inc(amp_step, 1)
            dve.wait_ge(amp_step, 2)
            nc.vector.tensor_reduce(power_sum[:, :], power[:, :], AX.X, ALU.add).then_inc(amp_step, 1)
            dve.wait_ge(amp_step, 3)
            nc.vector.tensor_scalar(power_den[:, :], power_sum[:, :], FFN_EPS, None, ALU.add).then_inc(amp_step, 1)
            dve.wait_ge(amp_step, 4)
            nc.vector.reciprocal(power_rec[:, :], power_den[:, :]).then_inc(amp_step, 1)
            dve.wait_ge(amp_step, 5)
            nc.vector.tensor_scalar(mix[:, :], power[:, :], power_rec[:, 0:1], escale[:, 0:1],
                                    ALU.mult, ALU.mult).then_inc(amp_step, 1)

            def yT(b):
                n = parity(b)
                dve.wait_ge(yT_hi_done, at(b, 1, 1))
                nc.vector.tensor_tensor(yT_lo[n][:, :, :].rearrange("p c s -> p (c s)"), ps_a[:, 0:KC * S],
                                        f32(yT_hi[n][:, :, :]).rearrange("p c s -> p (c s)"),
                                        ALU.subtract).then_inc(yT_lo_done, 1)

            def choose(b):
                n = parity(b)
                wait_alone(dve, logits_done, at(b, 1, 1))
                nc.vector.max(top8[n][:, :], logits[n][:, 0:E]).then_inc(top8_done, 1)
                dve.wait_ge(top8_done, at(b, 1, 1))
                nc.vector.tensor_scalar(neg_top[n][:, :], top8[n][:, 0:1], -1.0, None,
                                        ALU.mult).then_inc(neg_top_done, 1)
                nc.vector.tensor_copy(best4[n][:, 0:TOPK], top8[n][:, 0:TOPK]).then_inc(best4_done, 1)
                wait_alone(dve, best4_done, at(b, 1, 1))
                nc.vector.match_replace(replaced[n][:, :], best4[n][:, :], logits[n][:, :],
                                        TAKEN).then_inc(replaced_done, 1)

            def sum_chosen(b):
                n = parity(b)
                dve.wait_ge(replaced_done, at(b, 1, 1))
                dve.wait_ge(exp_done, at(b, 1, 1))
                nc.vector.scalar_tensor_tensor(out=chosen[n][:, :], in0=replaced[n][:, 0:E], scalar=BORDER,
                                               in1=expo[n][:, :], op0=ALU.is_lt, op1=ALU.mult,
                                               accum_out=chosen_sum[n][:, 0:1]).then_inc(chosen_done, 1)
                dve.wait_ge(chosen_done, at(b, 1, 1))
                nc.vector.tensor_scalar(coeff_den[n][:, :], exp_sum[n][:, :], FFN_EPS, chosen_sum[n][:, 0:1],
                                        ALU.mult, ALU.add).then_inc(coeff_den_done, 1)
                dve.wait_ge(coeff_den_done, at(b, 1, 1))
                nc.vector.reciprocal(coeff_rec[n][:, :], coeff_den[n][:, :]).then_inc(coeff_rec_done, 1)

            def weigh(b):
                n = parity(b)
                dve.wait_ge(coeff_ps, at(b, 1, 1))
                dve.wait_ge(coeff_rec_done, at(b, 1, 1))
                nc.vector.tensor_scalar(coeff[n][:, :], ps_a[:, E + S:E + S + K], coeff_rec[n][:, 0:1], None,
                                        ALU.mult).then_inc(coeff_done, 1)

            def gate(b, half):
                dve.wait_ge(tanh_done, at(b, 2, half + 1))
                nc.vector.scalar_tensor_tensor(out=gated[half][:, :], in0=tanh_g[half][:, :], scalar=1.0,
                                               in1=ps_gate[:, :], op0=ALU.add,
                                               op1=ALU.mult).then_inc(gated_done, 1)

            def basis(b, half):
                n = parity(b)
                dve.wait_ge(gated_done, at(b, 2, half + 1))
                dve.wait_ge(up_ps, at(b, 2, half + 1))
                dve.wait_ge(coeff_done, at(b, 1, 1))
                wait(dve, z_done, b, 1, -1)
                for k in range(HALF_K):
                    t = nc.vector.scalar_tensor_tensor(
                        out=bases[n][:, half * HALF_K + k, :], in0=ps_up[:, k * I:(k + 1) * I],
                        scalar=coeff[n][:, half * HALF_K + k:half * HALF_K + k + 1],
                        in1=gated[half][:, k * I:(k + 1) * I], op0=ALU.mult, op1=ALU.mult)
                t.then_inc(bases_done, 1)

            def shared_basis(b):
                n = parity(b)
                dve.wait_ge(tanh_s_done, at(b, 1, 1))
                nc.vector.scalar_tensor_tensor(out=gated_s[:, :], in0=tanh_s[:, :], scalar=1.0,
                                               in1=ps_gate[:, 0:SI], op0=ALU.add,
                                               op1=ALU.mult).then_inc(gated_s_done, 1)
                dve.wait_ge(gated_s_done, at(b, 1, 1))
                nc.vector.tensor_tensor(shared[n][:, :], ps_gate[:, SI:2 * SI], gated_s[:, :],
                                        ALU.mult).then_inc(shared_done, 1)

            def hT(b):
                n = parity(b)
                dve.wait_ge(hT_hi_done, at(b, 1, 1))
                nc.vector.scalar_tensor_tensor(out=hT_lo[n][:, :, :].rearrange("p c s -> p (c s)"),
                                               in0=ps_b[:, 0:3 * S], scalar=0.5,
                                               in1=f32(hT_hi[n][:, :, :]).rearrange("p c s -> p (c s)"),
                                               op0=ALU.mult, op1=ALU.subtract).then_inc(hT_lo_done, 1)

            def output(b):
                n = parity(b)
                dve.wait_ge(out_ps, at(b, 1, 1))
                if isinstance(b, tuple) or b >= 2:
                    dve.wait_ge(out_stored[n], by_parity(shift(b, -2)))
                nc.vector.tensor_tensor(out_sb[n][:, :], ps_b[:, 0:D], row(rows, b),
                                        ALU.add).then_inc(out_done, 1)

            def step(b, n):
                e, f, g = shift(b, -1), shift(b, -2), shift(b, -3)
                now, router, ffn, end = has(n, 0), has(n, -1), has(n, -2), has(n, -3)
                ahead, ahead2 = has(n, 1), has(n, 2)
                if router:
                    residual(e)
                    moments2_of(e)
                if ahead2:
                    moments_of(shift(b, 2))
                if router:
                    normalize2(e)
                if ahead2:
                    normalize(shift(b, 2))
                if ffn:
                    gate(f, 0)
                if ahead2:
                    k_lo(shift(b, 2))
                    q_lo(shift(b, 2))
                if router:
                    yT(e)
                if n == 1:
                    for piece in range(3, 7):
                        weight_lo(piece)
                if ffn:
                    basis(f, 0)
                if end:
                    hT(g)
                if router:
                    choose(e)
                if ahead:
                    maxima(shift(b, 1), 0)
                if ffn:
                    gate(f, 1)
                if router:
                    sum_chosen(e)
                if ahead:
                    maxima(shift(b, 1), 1)
                if ffn:
                    basis(f, 1)
                if now:
                    divide(b)
                if ahead:
                    maxima(shift(b, 1), 2)
                if router:
                    weigh(e)
                if end:
                    output(g)
                if ahead:
                    maxima(shift(b, 1), 3)
                if now:
                    attnT(b)
                if ahead:
                    split_max(shift(b, 1))
                if ffn:
                    shared_basis(f)

            run(dve, step)


_INS = ['x', 'ctx_512', 'L0_xattn_Wc', 'L0_xattn_bc', 'L0_ffn_w_router', 'L0_ffn_w_gate', 'L0_ffn_w_up',
        'L0_ffn_w_down', 'L0_ffn_amplitudes', 'L0_ffn_expert_scale', 'L0_ffn_shared_w_gate',
        'L0_ffn_shared_w_up', 'L0_ffn_shared_w_down']
_OUT = ((16, 128, 256), 'float32')


def kernel(**inputs):
    import numpy as _np
    import concourse.bacc as _bacc
    from concourse import mybir as _mybir
    from concourse.bass_utils import run_bass_kernel_spmd as _run

    nc = _bacc.Bacc("TRN2", target_bir_lowering=False, num_devices=1)
    arrays, args = {}, []
    for name in _INS:
        a = _np.ascontiguousarray(inputs[name])
        arrays[f"in_{name}_dram"] = a
        args.append(nc.dram_tensor(f"in_{name}_dram", a.shape, _mybir.dt.from_np(a.dtype), kind="ExternalInput").ap())
    args.append(nc.dram_tensor("out_0_dram", _OUT[0], _mybir.dt.from_np(_np.dtype(_OUT[1])),
                               kind="ExternalOutput").ap())
    build(nc, *args)
    r = _run(nc, [arrays], core_ids=[0])
    return r.results[0]["out_0_dram"]
```

```python
from contextlib import ExitStack

import concourse.bass as bass
from concourse import mybir

F32 = mybir.dt.float32
F32R = mybir.dt.float32r
ALU = mybir.AluOpType
ACT = mybir.ActivationFunctionType
AX = mybir.AxisListType

P = 128
HEADS = 16
GROUPS = 4
PER_GROUP = HEADS // GROUPS
DH = 16
VW = DH + 1
TOPK = 4
LN_EPS = 1e-5
FFN_EPS = 1e-8
SCORE_SCALE = DH ** -0.5
SPARE, TAKEN, BORDER = -3.0e38, -3.3e38, -3.2e38


def build(nc, x, ctx_in, wc, bc, w_router, w_gate, w_up, w_down, amplitudes, expert_scale,
          shared_gate, shared_up, shared_down, out):
    B, S, D = x.shape
    T = ctx_in.shape[1]
    DC = ctx_in.shape[2]
    E = w_router.shape[1]
    K = amplitudes.shape[1]
    I = w_down.shape[0]
    SI = shared_down.shape[0]
    assert (S, T, D, DC, E, I, SI, K) == (P, P, 2 * P, GROUPS * DH, P, P, 2 * P, 8)
    KC = D // P
    HALF_K = K // 2
    UP0, SG0, RT0 = K * I, 2 * K * I, 2 * K * I + 2 * SI
    WCOLS = RT0 + E
    WD0 = KC * WCOLS
    WALL = WD0 + 3 * D
    CONSTS = 1 + 14
    FIRST, LAST = 4, B - 3
    assert (LAST - FIRST + 1) % 2 == 0

    LO, MAX = 2 * DH, 3 * DH

    with ExitStack() as stack:
        def sb(name, shape, dt=F32):
            return stack.enter_context(nc.sbuf_tensor(name, shape, dt))

        def sem(name):
            return stack.enter_context(nc.semaphore(name))

        def two(name, shape, dt=F32):
            return [sb(f"{name}{n}", shape, dt) for n in range(2)]

        def f32(ap):
            return ap.bitcast(F32)

        rows = sb("rows", [P, B, D])
        ctx_sb = sb("ctx_sb", [P, B, DC])
        ident_f = sb("ident_f", [P, P])
        ident_r = sb("ident_r", [P, P], F32R)
        zeros_r = sb("zeros_r", [P, 4 * P], F32R)
        neg_half = sb("neg_half", [P, 1])
        wc_sb = sb("wc_sb", [P, 2, D])
        wcT_hi = sb("wcT_hi", [P, 2, D], F32R)
        wcT_lo = sb("wcT_lo", [P, 2, D], F32R)
        bias_bc = sb("bias_bc", [P, D])
        w_all = sb("w_all", [P, WALL])
        w_hi = sb("w_hi", [P, WALL], F32R)
        w_lo = sb("w_lo", [P, WALL], F32R)
        amp = sb("amp", [P, K, 2])
        amp_sq = sb("amp_sq", [P, K, 2])
        power = sb("power", [P, K])
        power_sum = sb("power_sum", [P, 1])
        power_den = sb("power_den", [P, 1])
        power_rec = sb("power_rec", [P, 1])
        escale = sb("escale", [P, 1])
        mix = sb("mix", [P, K])

        stats = two("stats", [P, 6])
        moments = two("moments", [P, 2])
        var_eps = two("var_eps", [P, 1])
        rstd = two("rstd", [P, 1])
        normed = two("normed", [P, D])
        stats2 = two("stats2", [P, 6])
        moments2 = two("moments2", [P, 2])
        var_eps2 = two("var_eps2", [P, 1])
        rstd2 = two("rstd2", [P, 1])
        normed2 = two("normed2", [P, D])
        x_bias = two("x_bias", [P, D])
        q_parts = two("q_parts", [P, 8, 2, 4 * DH], F32R)
        k_parts = two("k_parts", [P, 2, 2, 4 * DH], F32R)
        v_ones = two("v_ones", [P, GROUPS, VW])
        qT = two("qT", [P, 2, PER_GROUP, S], F32R)
        kT = two("kT", [P, 2, 2, T], F32R)
        row_max = two("row_max", [P, 2, PER_GROUP, 2])
        probs = [sb(f"probs{u}", [P, PER_GROUP, S]) for u in range(GROUPS)]
        den_rec = two("den_rec", [P, HEADS])
        attn = two("attn", [P, HEADS, DH])
        attnT_hi = two("attnT_hi", [P, KC, S], F32R)
        attnT_lo = two("attnT_lo", [P, KC, S], F32R)

        yT_hi = two("yT_hi", [P, KC, S], F32R)
        yT_lo = two("yT_lo", [P, KC, S], F32R)
        logits = two("logits", [P, E + TOPK])
        top8 = two("top8", [P, 8])
        best4 = two("best4", [P, 8])
        neg_top = two("neg_top", [P, 1])
        replaced = two("replaced", [P, E + TOPK])
        expo = two("expo", [P, E])
        exp_sum = two("exp_sum", [P, 1])
        chosen = two("chosen", [P, E])
        chosen_sum = two("chosen_sum", [P, 1])
        coeff_den = two("coeff_den", [P, 1])
        coeff_rec = two("coeff_rec", [P, 1])
        chosenT = two("chosenT", [P, S])
        coeff = two("coeff", [P, K])
        tanh_g = two("tanh_g", [P, HALF_K * I])
        gated = two("gated", [P, HALF_K * I])
        bases = two("bases", [P, K, I])
        sum4 = sb("sum4", [P, 4, I])
        sum2 = sb("sum2", [P, 2, I])
        zsum = two("zsum", [P, I])
        tanh_s = sb("tanh_s", [P, SI])
        gated_s = sb("gated_s", [P, SI])
        shared = two("shared", [P, SI])
        hT_hi = two("hT_hi", [P, 3, S], F32R)
        hT_lo = two("hT_lo", [P, 3, S], F32R)
        out_sb = two("out_sb", [P, D])

        bank = [stack.enter_context(nc.psum_tensor(f"bank{n}", [P, 512], F32)) for n in range(8)]
        ps_score, ps_gate, ps_up, ps_max = bank[0:2], bank[2], bank[3], bank[4]
        ps_pv, ps_a, ps_b = bank[5], bank[6], bank[7]

        def qT_bank(b, pair):
            if pair == 0:
                return ps_max
            return ps_score[1] if isinstance(b, int) and b == 0 else ps_b

        def is_last(b):
            return isinstance(b, int) and b >= B - 2

        def gate_bank(b, half):
            return ps_score[1] if is_last(b) and half == 1 else ps_gate

        def up_bank(b, half):
            return ps_max if is_last(b) and half == 1 else ps_up

        def shared_bank(b):
            return ps_score[0] if is_last(b) else ps_gate

        def qmT_bank(b, pair):
            return ps_a if isinstance(b, int) and b == 0 and pair == 1 else ps_max

        def max_bank(b, part):
            return (ps_gate, ps_pv, ps_a, ps_max)[part] if isinstance(b, int) and b == 0 else ps_max

        x_loaded = [sem(f"x_loaded{n}") for n in range(2)]
        ctx_loaded = [sem(f"ctx_loaded{n}") for n in range(2)]
        wc_loaded, bias_loaded = sem("wc_loaded"), sem("bias_loaded")
        amp_loaded = sem("amp_loaded")
        w_loaded = [sem(f"w_loaded{n}") for n in range(7)]
        zeroed, ident_made, ident_r_made, zeros_made = (
            sem("zeroed"), sem("ident_made"), sem("ident_r_made"), sem("zeros_made"))
        consts_made = sem("consts_made")
        wcT_ps, wcT_hi_made, wcT_made = sem("wcT_ps"), sem("wcT_hi_made"), sem("wcT_made")
        amp_step = sem("amp_step")
        w_hi_done, w_lo_dve, w_lo_pool = sem("w_hi_done"), sem("w_lo_dve"), sem("w_lo_pool")
        stats_done, moments_done, var_done, rstd_done, normed_done = (
            sem("stats_done"), sem("moments_done"), sem("var_done"), sem("rstd_done"), sem("normed_done"))
        x_bias_done = sem("x_bias_done")
        q_hi_done, q_lo_done, k_hi_done, k_lo_done, v_done = (
            sem("q_hi_done"), sem("q_lo_done"), sem("k_hi_done"), sem("k_lo_done"), sem("v_done"))
        stats2_done, moments2_done, var2_done, rstd2_done, normed2_done = (
            sem("stats2_done"), sem("moments2_done"), sem("var2_done"), sem("rstd2_done"), sem("normed2_done"))
        qT_ps, qT_done = sem("qT_ps"), sem("qT_done")
        kT_ps, kT_done = sem("kT_ps"), sem("kT_done")
        max_ps, max_done = sem("max_ps"), sem("max_done")
        max_hi_done, max_lo_done = sem("max_hi_done"), sem("max_lo_done")
        qmT_ps, qmT_done = sem("qmT_ps"), sem("qmT_done")
        score_ps, probs_done, pv_ps = sem("score_ps"), sem("probs_done"), sem("pv_ps")
        den_rec_done, attn_done, attnT_ps, attnT_hi_done, attnT_lo_done, proj_ps, x1_done = (
            sem("den_rec_done"), sem("attn_done"), sem("attnT_ps"), sem("attnT_hi_done"),
            sem("attnT_lo_done"), sem("proj_ps"), sem("x1_done"))

        yT_ps, yT_hi_done, yT_lo_done = sem("yT_ps"), sem("yT_hi_done"), sem("yT_lo_done")
        route_ps, logits_done, top8_done, neg_top_done, best4_done = (
            sem("route_ps"), sem("logits_done"), sem("top8_done"), sem("neg_top_done"), sem("best4_done"))
        exp_done, replaced_done, chosen_done, coeff_den_done, coeff_rec_done = (
            sem("exp_done"), sem("replaced_done"), sem("chosen_done"), sem("coeff_den_done"),
            sem("coeff_rec_done"))
        chosenT_ps, chosenT_done, coeff_ps, coeff_done = (
            sem("chosenT_ps"), sem("chosenT_done"), sem("coeff_ps"), sem("coeff_done"))
        gate_ps, up_ps, tanh_done, gated_done, bases_done = (
            sem("gate_ps"), sem("up_ps"), sem("tanh_done"), sem("gated_done"), sem("bases_done"))
        sum_step, z_done = sem("sum_step"), sem("z_done")
        shared_ps, tanh_s_done, gated_s_done, shared_done = (
            sem("shared_ps"), sem("tanh_s_done"), sem("gated_s_done"), sem("shared_done"))
        hT_ps, hT_hi_done, hT_lo_done, out_ps, out_done = (
            sem("hT_ps"), sem("hT_hi_done"), sem("hT_lo_done"), sem("out_ps"), sem("out_done"))
        out_stored = [sem(f"out_stored{n}") for n in range(2)]

        block = stack.enter_context(nc.Block())

        def parity(b):
            return (FIRST + b[1]) % 2 if isinstance(b, tuple) else b % 2

        def at(b, per=1, plus=0):
            if isinstance(b, tuple):
                return b[0] * (2 * per) + (per * (FIRST + b[1]) + plus)
            return per * b + plus

        def by_parity(b):
            if isinstance(b, tuple):
                return b[0] * 16 + 16 * ((FIRST + b[1]) // 2 + 1)
            return 16 * (b // 2 + 1)

        def shift(b, by):
            return (b[0], b[1] + by) if isinstance(b, tuple) else b + by

        def row(t, b):
            if isinstance(b, tuple):
                return t[:, bass.ds(b[0] * 2 + (FIRST + b[1]), 1), :].rearrange("p a d -> p (a d)")
            return t[:, b, :]

        def keys_of(b, a):
            return row(ctx_sb, b)[:, 2 * DH * a:2 * DH * (a + 1)].rearrange("p (r d) -> p r d", r=2)

        def keys_twice(b, a):
            c = row(ctx_sb, b)[:, 2 * DH * a:2 * DH * (a + 1)]
            return c.rearrange("p (r u d) -> p r u d", r=2, u=1).to_broadcast([P, 2, 2, DH])

        def heads_of(t):
            return t[:, :].rearrange("p (a t d) -> p a t d", a=2, d=DH)

        def q_place(n, part):
            return q_parts[n][:, :, :, part * DH:(part + 1) * DH].rearrange("p t a d -> p a t d")

        def group_of(u):
            return 2 * (u % 2) + u // 2

        def run(eng, step):
            for b in range(FIRST):
                step(b, b)
            with eng.Fori(0, (LAST - FIRST + 1) // 2) as r:
                for n in range(2):
                    step((r, n), None)
            for b in range(LAST + 1, B + 3):
                step(b, b)

        def has(n, by):
            return n is None or 0 <= n + by < B

        def wait(eng, s, b, per=1, plus=0):
            v = at(b, per, plus)
            if isinstance(b, tuple) or v > 0:
                eng.wait_ge(s, v)

        def wait_alone(eng, s, v):
            if not isinstance(v, int):
                v = eng.to_reg(v)
            eng.wait_ge(consts_made, CONSTS)
            if not isinstance(v, int) or v > 0:
                eng.wait_ge(s, v)

        w_view = w_all[:, 0:WD0].rearrange("p (c n) -> p c n", c=KC)
        w_hi_view = w_hi[:, 0:WD0].rearrange("p (c n) -> p c n", c=KC)
        w_lo_view = w_lo[:, 0:WD0].rearrange("p (c n) -> p c n", c=KC)

        def w_piece(n, t, view):
            if n < 5:
                c0, width = ((RT0, E), (0, K * I), (UP0, K * I), (SG0, SI), (SG0 + SI, SI))[n]
                return view[:, :, c0:c0 + width]
            if n == 5:
                return t[:, WD0:WD0 + D].rearrange("p (c n) -> p c n", c=1)
            return t[:, WD0 + D:WALL].rearrange("p (c n) -> p c n", c=2)

        w_sources = [w_router, w_gate, w_up, shared_gate, shared_up, w_down, shared_down]
        WARM = {"loads": 12, "qT 0": 3, "maxima 0": 5, "qmT 0": 3, "gate 0": 4, "up 0": 4, "gate 1": 3,
                "up 1": 3, "shared": 2, "down": 2, "last sum": 10, "last hT": 7}
        ON_POOL = (1, 2)

        @block.sync
        def _(sp):
            def load(b):
                n = parity(b)
                sp.dma_start(row(rows, b), dram_row(x, b)).then_inc(x_loaded[n], 16)
                sp.dma_start(row(ctx_sb, b), dram_row(ctx_in, b)).then_inc(ctx_loaded[n], 16)

            def dram_row(t, b):
                if isinstance(b, tuple):
                    return t[bass.ds(b[0] * 2 + (FIRST + b[1]), 1), :, :].rearrange("a p d -> (a p) d")
                return t[b]

            def load_weights(n):
                src = w_sources[n]
                sp.dma_start(w_piece(n, w_all, w_view),
                             src.rearrange("(c p) n -> p c n", p=P)).then_inc(w_loaded[n], 16)

            def load_next(b):
                before = shift(b, -2)
                sp.wait_ge(x_loaded[parity(b)], by_parity(before))
                sp.wait_ge(ctx_loaded[parity(b)], by_parity(before))
                load(b)

            for b in range(2):
                load(b)
            sp.dma_start(wc_sb[:, :, :], wc.rearrange("(m p) d -> p m d", p=P)).then_inc(wc_loaded, 16)
            for n in range(3):
                load_weights(n)
            for b in range(2, 4):
                load_next(b)
            for n in range(3, 7):
                load_weights(n)
            for b in range(4, FIRST + 2):
                load_next(b)
            with sp.Fori(0, (LAST - FIRST + 1) // 2) as r:
                for n in range(2):
                    load_next((r, n + 2))

            def store(b, n):
                sp.wait_ge(out_done, at(b, 1, 1))
                if isinstance(b, tuple):
                    dst = out[bass.ds(b[0] * 2 + (FIRST + b[1]), 1), :, :].rearrange("a p d -> (a p) d")
                else:
                    dst = out[b]
                sp.dma_start(dst, out_sb[parity(b)][:, :]).then_inc(out_stored[parity(b)], 16)

            for b in range(FIRST):
                store(b, b)
            with sp.Fori(0, (LAST - FIRST + 1) // 2) as r:
                for n in range(2):
                    store((r, n), None)
            for b in range(LAST + 1, B):
                store(b, b)
            for n in range(2):
                sp.wait_ge(out_stored[n], 16 * (B // 2))

        @block.gpsimd
        def _(pool):
            nc.gpsimd.memset(ident_f[:, :], 0.0).then_inc(zeroed, 1)
            pool.wait_ge(zeroed, 1)
            nc.gpsimd.affine_select(out=ident_f[:, :], in_=ident_f[:, :], compare_op=ALU.not_equal,
                                    fill=1.0, base=0, pattern=[[-1, P]],
                                    channel_multiplier=1).then_inc(ident_made, 1)
            nc.gpsimd.memset(neg_half[:, :], -0.5).then_inc(consts_made, 1)

            def rsqrt(b):
                n = parity(b)
                pool.wait_ge(var_done, at(b, 1, 1))
                nc.gpsimd.tensor_tensor(rstd[n][:, :], var_eps[n][:, :], neg_half[:, :],
                                        ALU.pow).then_inc(rstd_done, 1)

            def rsqrt2(b):
                n = parity(b)
                pool.wait_ge(var2_done, at(b, 1, 1))
                nc.gpsimd.tensor_tensor(rstd2[n][:, :], var_eps2[n][:, :], neg_half[:, :],
                                        ALU.pow).then_inc(rstd2_done, 1)

            def add_bias(b):
                n = parity(b)
                pool.wait_ge(x_loaded[n], by_parity(b))
                wait(pool, x1_done, b, 1, -1)
                nc.gpsimd.tensor_tensor(x_bias[n][:, :], row(rows, b), bias_bc[:, :],
                                        ALU.add).then_inc(x_bias_done, 1)

            def k_lo(b):
                n = parity(b)
                pool.wait_ge(k_hi_done, at(b, 1, 1))
                for a in range(2):
                    t = nc.gpsimd.tensor_tensor(k_parts[n][:, :, a, LO:LO + DH], keys_of(b, a),
                                                f32(k_parts[n][:, :, a, 0:DH]), ALU.subtract)
                t.then_inc(k_lo_done, 1)

            def weights_lo(n):
                pool.wait_ge(w_hi_done, n + 1)
                nc.gpsimd.tensor_tensor(w_piece(n, w_lo, w_lo_view), w_piece(n, w_all, w_view),
                                        f32(w_piece(n, w_hi, w_hi_view)), ALU.subtract).then_inc(w_lo_pool, 1)

            def sum_bases(b):
                n = parity(b)
                pool.wait_ge(bases_done, at(b, 2, 2))
                nc.gpsimd.tensor_tensor(sum4[:, :, :], bases[n][:, 0:4, :], bases[n][:, 4:8, :],
                                        ALU.add).then_inc(sum_step, 1)
                pool.wait_ge(sum_step, at(b, 2, 1))
                nc.gpsimd.tensor_tensor(sum2[:, :, :], sum4[:, 0:2, :], sum4[:, 2:4, :],
                                        ALU.add).then_inc(sum_step, 1)
                pool.wait_ge(sum_step, at(b, 2, 2))
                nc.gpsimd.tensor_tensor(zsum[n][:, :], sum2[:, 0, :], sum2[:, 1, :],
                                        ALU.add).then_inc(z_done, 1)

            rsqrt(0)
            k_lo(0)
            rsqrt(1)
            k_lo(1)
            rsqrt(2)
            weights_lo(ON_POOL[0])
            pool.wait_ge(bias_loaded, 16)

            def step(b, n):
                if has(n, -1):
                    rsqrt2(shift(b, -1))
                if has(n, 2) and n != 0:
                    rsqrt(shift(b, 2))
                if has(n, 0):
                    add_bias(b)
                if has(n, 2):
                    k_lo(shift(b, 2))
                if n == 0:
                    weights_lo(ON_POOL[1])
                if has(n, -2) and shift(b, -2) != B - 1:
                    sum_bases(shift(b, -2))

            run(pool, step)

        @block.scalar
        def _(act):
            act.dma_start(bias_bc[:, :], bc.partition_broadcast(P)).then_inc(bias_loaded, 16)
            act.dma_start(amp[:, :, :], amplitudes).then_inc(amp_loaded, 16)
            act.dma_start(escale[:, :], expert_scale.rearrange("(e a) -> e a", a=1)).then_inc(amp_loaded, 16)

            def keys(b):
                n = parity(b)
                act.wait_ge(ctx_loaded[n], by_parity(b))
                wait_alone(act, kT_ps, at(b, 1, -1))
                for a in range(2):
                    t = nc.scalar.activation(
                        k_parts[n][:, :, a, 0:2 * DH].rearrange("p r (u d) -> p r u d", u=2),
                        keys_twice(b, a), ACT.Copy)
                t.then_inc(k_hi_done, 1)

            def values(b):
                n = parity(b)
                wait_alone(act, pv_ps, at(b, 4, -4))
                nc.scalar.activation(v_ones[n][:, :, 0:DH], row(ctx_sb, b).rearrange("p (g d) -> p g d", g=GROUPS),
                                     ACT.Copy).then_inc(v_done, 1)

            def q_hi(b):
                n = parity(b)
                act.wait_ge(normed_done, at(b, 1, 1))
                wait(act, qmT_ps, b, 2, -2)
                for u in range(2):
                    t = nc.scalar.activation(q_place(n, 2 * u), heads_of(normed[n]), ACT.Copy)
                t.then_inc(q_hi_done, 1)

            def evacuate_qT(b, pair):
                n = parity(b)
                act.wait_ge(qT_ps, at(b, 2, pair + 1))
                nc.scalar.activation(qT[n][:, pair, :, :].rearrange("p j s -> p (j s)"), qT_bank(b, pair)[:, :],
                                     ACT.Copy).then_inc(qT_done, 1)

            def evacuate_kT(b):
                n = parity(b)
                act.wait_ge(kT_ps, at(b, 1, 1))
                src = ps_b[:, 0:2 * T].rearrange("p (a t) -> p a t", a=2)
                nc.scalar.activation(kT[n][0:64, :, 0, :], src[0:64, :, :], ACT.Copy)
                nc.scalar.activation(kT[n][64:128, :, 1, :], src[64:128, :, :], ACT.Copy).then_inc(kT_done, 1)

            def evacuate_qmT(b, pair):
                n = parity(b)
                act.wait_ge(qmT_ps, at(b, 2, pair + 1))
                nc.scalar.activation(qT[n][:, pair, :, :].rearrange("p j s -> p (j s)"),
                                     qmT_bank(b, pair)[:, :], ACT.Copy).then_inc(qmT_done, 1)

            def exps(b, u):
                act.wait_ge(score_ps, at(b, 4, u + 1))
                nc.scalar.activation(probs[u][:, :, :].rearrange("p j s -> p (j s)"), ps_score[u % 2][:, :],
                                     ACT.Exp, scale=SCORE_SCALE).then_inc(probs_done, 1)

            def attnT(b):
                n = parity(b)
                act.wait_ge(attnT_ps, at(b, 1, 1))
                nc.scalar.activation(attnT_hi[n][:, :, :].rearrange("p c s -> p (c s)"),
                                     ps_a[:, 0:KC * S], ACT.Copy).then_inc(attnT_hi_done, 1)

            def weight_hi(n):
                act.wait_ge(w_loaded[n], 16)
                nc.scalar.activation(w_piece(n, w_hi, w_hi_view), w_piece(n, w_all, w_view),
                                     ACT.Copy).then_inc(w_hi_done, 1)

            act.wait_ge(ident_made, 1)
            nc.scalar.activation(ident_r[:, :], ident_f[:, :], ACT.Copy).then_inc(ident_r_made, 1)
            keys(0)
            q_hi(0)
            evacuate_qT(0, 0)
            evacuate_kT(0)
            evacuate_qT(0, 1)
            act.wait_ge(wcT_ps, 1)
            nc.scalar.activation(wcT_hi[:, :, :].rearrange("p c n -> p (c n)"), ps_score[0][:, :],
                                 ACT.Copy).then_inc(wcT_hi_made, 1)
            keys(1)
            q_hi(1)
            values(0)
            for n in (0, 1):
                weight_hi(n)
            for pair in range(2):
                evacuate_qmT(0, pair)

            def yT(b):
                n = parity(b)
                act.wait_ge(yT_ps, at(b, 1, 1))
                nc.scalar.activation(yT_hi[n][:, :, :].rearrange("p c s -> p (c s)"),
                                     ps_a[:, 0:KC * S], ACT.Copy).then_inc(yT_hi_done, 1)

            def copy_logits(b):
                n = parity(b)
                act.wait_ge(route_ps, at(b, 1, 1))
                nc.scalar.activation(logits[n][:, 0:E], ps_a[:, 0:E], ACT.Copy).then_inc(logits_done, 1)

            def exp_logits(b):
                n = parity(b)
                act.wait_ge(neg_top_done, at(b, 1, 1))
                nc.scalar.activation(expo[n][:, :], logits[n][:, 0:E], ACT.Exp, bias=neg_top[n][:, 0:1],
                                     accum_out=exp_sum[n][:, 0:1]).then_inc(exp_done, 1)

            def copy_chosenT(b):
                n = parity(b)
                act.wait_ge(chosenT_ps, at(b, 1, 1))
                nc.scalar.activation(chosenT[n][:, :], ps_a[:, E:E + S], ACT.Copy).then_inc(chosenT_done, 1)

            def tanh(b, half):
                act.wait_ge(gate_ps, at(b, 2, half + 1))
                if b == B - 2 and half == 1:
                    act.wait_ge(gated_done, at(b, 2, 0))
                nc.scalar.activation(tanh_g[half][:, :], gate_bank(b, half)[:, :], ACT.Tanh,
                                     scale=0.5).then_inc(tanh_done, 1)

            def tanh_shared(b):
                act.wait_ge(shared_ps, at(b, 1, 1))
                if is_last(b):
                    act.wait_ge(gated_s_done, b)
                nc.scalar.activation(tanh_s[:, :], shared_bank(b)[:, 0:SI], ACT.Tanh,
                                     scale=0.5).then_inc(tanh_s_done, 1)

            def hT(b):
                n = parity(b)
                act.wait_ge(hT_ps, at(b, 1, 1))
                nc.scalar.activation(hT_hi[n][:, :, :].rearrange("p c s -> p (c s)"), ps_b[:, 0:3 * S],
                                     ACT.Copy, scale=0.5).then_inc(hT_hi_done, 1)

            def step(b, n):
                e, f, g = shift(b, -1), shift(b, -2), shift(b, -3)
                now, route, ffn, end = has(n, 0), has(n, -1), has(n, -2), has(n, -3)
                ahead, ahead2 = has(n, 1), has(n, 2)
                if ahead:
                    evacuate_qT(shift(b, 1), 0)
                if now:
                    exps(b, 0)
                    exps(b, 1)
                if ahead:
                    evacuate_kT(shift(b, 1))
                f_last = ffn and is_last(f)
                if f_last:
                    tanh_shared(f)
                if ffn:
                    tanh(f, 0)
                if ahead2:
                    keys(shift(b, 2))
                    q_hi(shift(b, 2))
                if route:
                    yT(e)
                if now:
                    exps(b, 2)
                if ahead:
                    evacuate_qT(shift(b, 1), 1)
                if now:
                    exps(b, 3)
                if n == 0:
                    for piece in (2, 3, 4):
                        weight_hi(piece)
                if n == 1:
                    for piece in (5, 6):
                        weight_hi(piece)
                if ahead:
                    values(shift(b, 1))
                if end:
                    hT(g)
                if route:
                    copy_logits(e)
                if ffn:
                    tanh(f, 1)
                if route:
                    exp_logits(e)
                    copy_chosenT(e)
                if ahead:
                    evacuate_qmT(shift(b, 1), 0)
                if ffn and not f_last:
                    tanh_shared(f)
                if now:
                    attnT(b)
                if ahead:
                    evacuate_qmT(shift(b, 1), 1)

            run(act, step)

        @block.tensor
        def _(pe):
            def transpose_q(b, pair):
                n = parity(b)
                if pair == 0:
                    pe.wait_ge(q_lo_done, at(b, 1, 1))
                    if isinstance(b, int) and b == 1:
                        pe.wait_ge(qmT_done, 1)
                    else:
                        wait(pe, qmT_done, b, 2)
                elif isinstance(b, tuple) or b > 0:
                    pe.wait_ge(kT_done, at(b, 1, 1))
                for j in range(PER_GROUP):
                    src = q_parts[n][:, PER_GROUP * pair + j, :, :].rearrange("p a d -> p (a d)")
                    t = nc.tensor.transpose(qT_bank(b, pair)[:, j * S:(j + 1) * S].bitcast(F32R), src, ident_r[:, :])
                t.then_inc(qT_ps, 1)

            def transpose_k(b):
                n = parity(b)
                pe.wait_ge(k_lo_done, at(b, 1, 1))
                wait(pe, out_done, b, 1, -4)
                for pair in range(2):
                    t = nc.tensor.transpose(ps_b[:, pair * T:(pair + 1) * T].bitcast(F32R),
                                            k_parts[n][:, pair, :, :].rearrange("p a d -> p (a d)"),
                                            ident_r[:, :])
                t.then_inc(kT_ps, 1)

            def max_scores(b, part):
                n, pair = parity(b), part // 2
                if part == 0:
                    pe.wait_ge(kT_done, at(b, 1, 1))
                elif isinstance(b, tuple) or b > 0:
                    pe.wait_ge(max_done, at(b, 4, part))
                if part == 2:
                    pe.wait_ge(qT_done, at(b, 2, 2))
                for u in range(2):
                    t = nc.tensor.matmul(max_bank(b, part)[:, 2 * T * u:2 * T * (u + 1)],
                                         qT[n][:, pair, 2 * (part % 2) + u, :],
                                         kT[n][:, pair, :, :].rearrange("p a t -> p (a t)"),
                                         start=True, stop=True)
                t.then_inc(max_ps, 1)

            def transpose_qm(b, pair):
                n = parity(b)
                pe.wait_ge(max_lo_done, at(b, 1, 1))
                if pair == 1 and (isinstance(b, tuple) or b > 0):
                    pe.wait_ge(qmT_done, at(b, 2, 1))
                for j in range(PER_GROUP):
                    src = q_parts[n][:, PER_GROUP * pair + j, :, :].rearrange("p a d -> p (a d)")
                    t = nc.tensor.transpose(qmT_bank(b, pair)[:, j * S:(j + 1) * S].bitcast(F32R), src,
                                            ident_r[:, :])
                t.then_inc(qmT_ps, 1)

            def scores(b, u):
                n, pair, a = parity(b), u // 2, u % 2
                if a == 0:
                    pe.wait_ge(qmT_done, at(b, 2, pair + 1))
                if u >= 2:
                    pe.wait_ge(probs_done, at(b, 4, u - 1))
                nc.tensor.matmul(ps_score[u % 2][:, :], kT[n][64 * a:64 * a + 64, pair, a, :],
                                 qT[n][64 * a:64 * a + 64, pair, :, :].rearrange("p j s -> p (j s)"),
                                 start=True, stop=True).then_inc(score_ps, 1)

            def values(b, u):
                pe.wait_ge(probs_done, at(b, 4, u + 1))
                g = group_of(u)
                if u == 0:
                    pe.wait_ge(v_done, at(b, 1, 1))
                    wait(pe, attn_done, b)
                for j in range(PER_GROUP):
                    h = PER_GROUP * g + j
                    t = nc.tensor.matmul(ps_pv[:, h * VW:(h + 1) * VW], probs[u][:, j, :],
                                         v_ones[parity(b)][:, g, :], start=True, stop=True)
                t.then_inc(pv_ps, 1)

            def transpose_attn(b):
                n = parity(b)
                pe.wait_ge(attn_done, at(b, 1, 1))
                wait(pe, coeff_done, b)
                for c in range(KC):
                    t = nc.tensor.transpose(ps_a[:, c * S:(c + 1) * S],
                                            attn[n][:, 8 * c:8 * c + 8, :].rearrange("p h d -> p (h d)"),
                                            ident_f[:, :])
                t.then_inc(attnT_ps, 1)

            def three_passes(dst, hi, lo, rhs_hi, rhs_lo, chunks):
                k = 0
                for c in range(chunks):
                    for l, r in ((hi, rhs_hi), (hi, rhs_lo), (lo, rhs_hi)):
                        t = nc.tensor.matmul(dst, l(c), r(c), start=(k == 0), stop=(k == 3 * chunks - 1))
                        k += 1
                return t

            def project(b):
                n = parity(b)
                pe.wait_ge(attnT_lo_done, at(b, 1, 1))
                three_passes(ps_a[:, 0:D], lambda c: attnT_hi[n][:, c, :], lambda c: attnT_lo[n][:, c, :],
                             lambda c: wcT_hi[:, c, :], lambda c: wcT_lo[:, c, :], KC).then_inc(proj_ps, 1)

            def keep_warm(count, dst=ps_up):
                for _ in range(count):
                    nc.tensor.matmul(dst[:, :], zeros_r[:, 0:P], zeros_r[:, :], start=True, stop=True)

            pe.wait_ge(zeros_made, 1)
            keep_warm(WARM["loads"])
            pe.wait_ge(ident_r_made, 1)
            transpose_q(0, 0)
            transpose_k(0)
            transpose_q(0, 1)
            pe.wait_ge(wc_loaded, 16)
            for c in range(KC):
                for m in range(2):
                    t = nc.tensor.transpose(ps_score[0][:, c * D + m * P:c * D + (m + 1) * P],
                                            wc_sb[:, m, c * P:(c + 1) * P], ident_f[:, :])
            t.then_inc(wcT_ps, 1)
            keep_warm(WARM["qT 0"])
            for part in range(4):
                max_scores(0, part)
            keep_warm(WARM["maxima 0"])
            for pair in range(2):
                transpose_qm(0, pair)
            keep_warm(WARM["qmT 0"])

            def transpose_y(b):
                n = parity(b)
                pe.wait_ge(normed2_done, at(b, 1, 1))
                for c in range(KC):
                    t = nc.tensor.transpose(ps_a[:, c * S:(c + 1) * S], normed2[n][:, c * P:(c + 1) * P],
                                            ident_f[:, :])
                t.then_inc(yT_ps, 1)

            def weights(b, dst, c0, width):
                n = parity(b)
                return three_passes(dst, lambda c: yT_hi[n][:, c, :], lambda c: yT_lo[n][:, c, :],
                                    lambda c: w_hi[:, c * WCOLS + c0:c * WCOLS + c0 + width],
                                    lambda c: w_lo[:, c * WCOLS + c0:c * WCOLS + c0 + width], KC)

            def route(b):
                pe.wait_ge(yT_lo_done, at(b, 1, 1))
                weights(b, ps_a[:, 0:E], RT0, E).then_inc(route_ps, 1)

            def transpose_chosen(b):
                pe.wait_ge(chosen_done, at(b, 1, 1))
                nc.tensor.transpose(ps_a[:, E:E + S], chosen[parity(b)][:, :],
                                    ident_f[:, :]).then_inc(chosenT_ps, 1)

            def mix_experts(b):
                pe.wait_ge(chosenT_done, at(b, 1, 1))
                nc.tensor.matmul(ps_a[:, E + S:E + S + K], chosenT[parity(b)][:, :], mix[:, :],
                                 start=True, stop=True).then_inc(coeff_ps, 1)

            def gate(b, half):
                if is_last(b):
                    if b == B - 1:
                        pe.wait_ge(gated_done, at(b, 2, half - 1))
                    elif half == 0:
                        pe.wait_ge(shared_done, b)
                elif half == 0:
                    wait(pe, shared_done, b)
                else:
                    pe.wait_ge(gated_done, at(b, 2, 1))
                weights(b, gate_bank(b, half)[:, :], half * HALF_K * I, HALF_K * I).then_inc(gate_ps, 1)

            def up(b, half):
                if is_last(b):
                    if b == B - 1:
                        pe.wait_ge(bases_done, at(b, 2, half - 1))
                    elif half == 0:
                        pe.wait_ge(bases_done, at(b, 2, 0))
                else:
                    wait(pe, bases_done, b, 2, half)
                weights(b, up_bank(b, half)[:, :], UP0 + half * HALF_K * I, HALF_K * I).then_inc(up_ps, 1)

            def shared_in(b):
                if not is_last(b):
                    pe.wait_ge(gated_done, at(b, 2, 2))
                elif b == B - 1:
                    pe.wait_ge(shared_done, b)
                weights(b, shared_bank(b)[:, :], SG0, 2 * SI).then_inc(shared_ps, 1)

            def transpose_h(b):
                n = parity(b)
                pe.wait_ge(z_done, at(b, 1, 1))
                pe.wait_ge(shared_done, at(b, 1, 1))
                if isinstance(b, tuple) or b + 4 < B:
                    pe.wait_ge(qT_done, at(b, 2, 10))
                elif b + 3 >= B:
                    pe.wait_ge(out_done, b)
                nc.tensor.transpose(ps_b[:, 0:S], zsum[n][:, :], ident_f[:, :])
                for c in range(2):
                    t = nc.tensor.transpose(ps_b[:, (c + 1) * S:(c + 2) * S], shared[n][:, c * P:(c + 1) * P],
                                            ident_f[:, :])
                t.then_inc(hT_ps, 1)

            def down(b):
                n = parity(b)
                pe.wait_ge(hT_lo_done, at(b, 1, 1))
                three_passes(ps_b[:, 0:D], lambda c: hT_hi[n][:, c, :], lambda c: hT_lo[n][:, c, :],
                             lambda c: w_hi[:, WD0 + c * D:WD0 + (c + 1) * D],
                             lambda c: w_lo[:, WD0 + c * D:WD0 + (c + 1) * D], 3).then_inc(out_ps, 1)

            def step(b, n):
                e, f, g = shift(b, -1), shift(b, -2), shift(b, -3)
                now, router, ffn, end, ahead = has(n, 0), has(n, -1), has(n, -2), has(n, -3), has(n, 1)
                first = n is not None and n < 2
                f_last = ffn and is_last(f)
                if ahead:
                    transpose_q(shift(b, 1), 0)
                if n == 0:
                    pe.wait_ge(wcT_made, 1)
                if now:
                    scores(b, 0)
                    scores(b, 1)
                if ahead:
                    transpose_k(shift(b, 1))
                if f_last:
                    shared_in(f)
                if n == 2:
                    pe.wait_ge(w_lo_pool, 1)
                if ffn:
                    gate(f, 0)
                if first:
                    keep_warm(WARM["gate 0"])
                if f_last and f == B - 1:
                    mix_experts(f)
                if now:
                    values(b, 0)
                    scores(b, 2)
                if ahead:
                    max_scores(shift(b, 1), 0)
                    transpose_q(shift(b, 1), 1)
                if router and not f_last:
                    transpose_y(e)
                if n == 2:
                    pe.wait_ge(w_lo_pool, 2)
                if ffn:
                    up(f, 0)
                if router and f_last:
                    transpose_y(e)
                if first:
                    keep_warm(WARM["up 0"])
                if ahead:
                    max_scores(shift(b, 1), 1)
                if now:
                    values(b, 1)
                    scores(b, 3)
                if n == B + 2:
                    keep_warm(WARM["last sum"], ps_pv)
                if end and not f_last:
                    transpose_h(g)
                if n == B + 2:
                    keep_warm(WARM["last hT"], ps_pv)
                if n == 1:
                    pe.wait_ge(w_lo_dve, 1)
                    pe.wait_ge(amp_step, 6)
                if router and not f_last:
                    route(e)
                if ahead:
                    max_scores(shift(b, 1), 2)
                if ffn:
                    gate(f, 1)
                if end and f_last:
                    transpose_h(g)
                if router and f_last:
                    route(e)
                if first:
                    keep_warm(WARM["gate 1"])
                if now:
                    values(b, 2)
                if ahead:
                    max_scores(shift(b, 1), 3)
                if ffn:
                    up(f, 1)
                if first:
                    keep_warm(WARM["up 1"])
                if end and f_last:
                    down(g)
                if router:
                    transpose_chosen(e)
                if now:
                    values(b, 3)
                if ahead:
                    transpose_qm(shift(b, 1), 0)
                if router and not f_last:
                    mix_experts(e)
                if n == 2:
                    pe.wait_ge(w_lo_dve, 3)
                if ffn and not f_last:
                    shared_in(f)
                if first:
                    keep_warm(WARM["shared"])
                if now:
                    transpose_attn(b)
                if ahead:
                    transpose_qm(shift(b, 1), 1)
                if first:
                    keep_warm(WARM["down"])
                if n == 3:
                    pe.wait_ge(w_lo_dve, 5)
                if end and not f_last:
                    down(g)
                if now:
                    project(b)

            run(pe, step)

        @block.vector
        def _(dve):
            def moments_of(b):
                n = parity(b)
                dve.wait_ge(x_loaded[n], by_parity(b))
                nc.vector.bn_stats(stats[n][:, :], row(rows, b)).then_inc(stats_done, 1)
                wait_alone(dve, stats_done, at(b, 1, 1))
                nc.vector.bn_aggr(moments[n][:, :], stats[n][:, :]).then_inc(moments_done, 1)
                dve.wait_ge(moments_done, at(b, 1, 1))
                nc.vector.tensor_scalar(var_eps[n][:, :], moments[n][:, 1:2], LN_EPS, None,
                                        ALU.add).then_inc(var_done, 1)

            def normalize(b):
                n = parity(b)
                dve.wait_ge(rstd_done, at(b, 1, 1))
                nc.vector.tensor_scalar(normed[n][:, :], row(rows, b), moments[n][:, 0:1], rstd[n][:, 0:1],
                                        ALU.subtract, ALU.mult).then_inc(normed_done, 1)

            def moments2_of(b):
                n = parity(b)
                wait_alone(dve, x1_done, at(b, 1, 1))
                nc.vector.bn_stats(stats2[n][:, :], row(rows, b)).then_inc(stats2_done, 1)
                wait_alone(dve, stats2_done, at(b, 1, 1))
                nc.vector.bn_aggr(moments2[n][:, :], stats2[n][:, :]).then_inc(moments2_done, 1)
                dve.wait_ge(moments2_done, at(b, 1, 1))
                nc.vector.tensor_scalar(var_eps2[n][:, :], moments2[n][:, 1:2], LN_EPS, None,
                                        ALU.add).then_inc(var2_done, 1)

            def normalize2(b):
                n = parity(b)
                dve.wait_ge(rstd2_done, at(b, 1, 1))
                nc.vector.tensor_scalar(normed2[n][:, :], row(rows, b), moments2[n][:, 0:1], rstd2[n][:, 0:1],
                                        ALU.subtract, ALU.mult).then_inc(normed2_done, 1)

            def q_lo(b):
                n = parity(b)
                dve.wait_ge(q_hi_done, at(b, 1, 1))
                nc.vector.memset(f32(q_parts[n][:, :, :, MAX:MAX + 2]), 0.0)
                nc.vector.tensor_tensor(q_place(n, 1), heads_of(normed[n]), f32(q_place(n, 0)),
                                        ALU.subtract).then_inc(q_lo_done, 1)

            def maxima(b, part):
                n = parity(b)
                dve.wait_ge(max_ps, at(b, 4, part + 1))
                dst = row_max[n][:, part // 2, 2 * (part % 2):2 * (part % 2) + 2, :].rearrange("p j a -> p (j a)")
                nc.vector.tensor_reduce(dst, max_bank(b, part)[:, :].rearrange("p (x t) -> p x t", t=T),
                                        AX.X, ALU.max).then_inc(max_done, 1)

            def split_max(b):
                n = parity(b)
                dve.wait_ge(max_done, at(b, 4, 4))
                maxima_of = row_max[n][:, :, :, :].rearrange("p r j a -> p (r j) a")
                hi, lo = q_parts[n][:, :, :, MAX], q_parts[n][:, :, :, MAX + 1]
                nc.vector.tensor_copy(hi, maxima_of).then_inc(max_hi_done, 1)
                dve.wait_ge(max_hi_done, at(b, 1, 1))
                nc.vector.tensor_tensor(lo, maxima_of, f32(hi), ALU.subtract).then_inc(max_lo_done, 1)

            def divide(b):
                n = parity(b)
                dve.wait_ge(pv_ps, at(b, 4, 4))
                pv = ps_pv[:, 0:HEADS * VW].rearrange("p (h w) -> p h w", w=VW)
                nc.vector.reciprocal(den_rec[n][:, :], pv[:, :, DH]).then_inc(den_rec_done, 1)
                dve.wait_ge(den_rec_done, at(b, 1, 1))
                nc.vector.tensor_tensor(
                    attn[n][:, :, :], pv[:, :, 0:DH],
                    den_rec[n][:, :].rearrange("p (h a) -> p h a", a=1).to_broadcast([P, HEADS, DH]),
                    ALU.mult).then_inc(attn_done, 1)

            def attnT(b):
                n = parity(b)
                dve.wait_ge(attnT_hi_done, at(b, 1, 1))
                nc.vector.tensor_tensor(attnT_lo[n][:, :, :].rearrange("p c s -> p (c s)"), ps_a[:, 0:KC * S],
                                        f32(attnT_hi[n][:, :, :]).rearrange("p c s -> p (c s)"),
                                        ALU.subtract).then_inc(attnT_lo_done, 1)

            def residual(b):
                n = parity(b)
                dve.wait_ge(proj_ps, at(b, 1, 1))
                dve.wait_ge(x_bias_done, at(b, 1, 1))
                nc.vector.tensor_tensor(row(rows, b), ps_a[:, 0:D], x_bias[n][:, :],
                                        ALU.add).then_inc(x1_done, 1)

            nc.vector.memset(f32(zeros_r[:, :]), 0.0).then_inc(zeros_made, 1)
            for n in range(2):
                nc.vector.memset(f32(q_parts[n][:, :, :, MAX + 2:4 * DH]), 0.0).then_inc(consts_made, 1)
                nc.vector.memset(f32(k_parts[n][:, :, :, MAX + 2:4 * DH]), 0.0).then_inc(consts_made, 1)
                nc.vector.memset(f32(k_parts[n][:, :, :, MAX:MAX + 2]), -1.0).then_inc(consts_made, 1)
                nc.vector.memset(f32(kT[n][:, :, :, :]), 0.0).then_inc(consts_made, 1)
                nc.vector.memset(v_ones[n][:, :, DH:VW], 1.0).then_inc(consts_made, 1)
                nc.vector.memset(logits[n][:, E:E + TOPK], SPARE).then_inc(consts_made, 1)
                nc.vector.memset(best4[n][:, TOPK:8], SPARE).then_inc(consts_made, 1)
            moments_of(0)
            normalize(0)
            q_lo(0)
            moments_of(1)
            normalize(1)
            for part in range(4):
                maxima(0, part)
            split_max(0)
            q_lo(1)
            dve.wait_ge(wcT_hi_made, 1)
            nc.vector.tensor_tensor(wcT_lo[:, :, :].rearrange("p c n -> p (c n)"), ps_score[0][:, :],
                                    f32(wcT_hi[:, :, :]).rearrange("p c n -> p (c n)"),
                                    ALU.subtract).then_inc(wcT_made, 1)
            moments_of(2)

            def weight_lo(n):
                dve.wait_ge(w_hi_done, n + 1)
                nc.vector.tensor_tensor(w_piece(n, w_lo, w_lo_view), w_piece(n, w_all, w_view),
                                        f32(w_piece(n, w_hi, w_hi_view)), ALU.subtract).then_inc(w_lo_dve, 1)

            weight_lo(0)

            dve.wait_ge(amp_loaded, 32)
            nc.vector.tensor_tensor(amp_sq[:, :, :], amp[:, :, :], amp[:, :, :], ALU.mult).then_inc(amp_step, 1)
            dve.wait_ge(amp_step, 1)
            nc.vector.tensor_reduce(power[:, :], amp_sq[:, :, :], AX.X, ALU.add).then_inc(amp_step, 1)
            dve.wait_ge(amp_step, 2)
            nc.vector.tensor_reduce(power_sum[:, :], power[:, :], AX.X, ALU.add).then_inc(amp_step, 1)
            dve.wait_ge(amp_step, 3)
            nc.vector.tensor_scalar(power_den[:, :], power_sum[:, :], FFN_EPS, None, ALU.add).then_inc(amp_step, 1)
            dve.wait_ge(amp_step, 4)
            nc.vector.reciprocal(power_rec[:, :], power_den[:, :]).then_inc(amp_step, 1)
            dve.wait_ge(amp_step, 5)
            nc.vector.tensor_scalar(mix[:, :], power[:, :], power_rec[:, 0:1], escale[:, 0:1],
                                    ALU.mult, ALU.mult).then_inc(amp_step, 1)

            def yT(b):
                n = parity(b)
                dve.wait_ge(yT_hi_done, at(b, 1, 1))
                nc.vector.tensor_tensor(yT_lo[n][:, :, :].rearrange("p c s -> p (c s)"), ps_a[:, 0:KC * S],
                                        f32(yT_hi[n][:, :, :]).rearrange("p c s -> p (c s)"),
                                        ALU.subtract).then_inc(yT_lo_done, 1)

            def choose(b):
                n = parity(b)
                wait_alone(dve, logits_done, at(b, 1, 1))
                nc.vector.max(top8[n][:, :], logits[n][:, 0:E]).then_inc(top8_done, 1)
                dve.wait_ge(top8_done, at(b, 1, 1))
                nc.vector.tensor_scalar(neg_top[n][:, :], top8[n][:, 0:1], -1.0, None,
                                        ALU.mult).then_inc(neg_top_done, 1)
                nc.vector.tensor_copy(best4[n][:, 0:TOPK], top8[n][:, 0:TOPK]).then_inc(best4_done, 1)
                wait_alone(dve, best4_done, at(b, 1, 1))
                nc.vector.match_replace(replaced[n][:, :], best4[n][:, :], logits[n][:, :],
                                        TAKEN).then_inc(replaced_done, 1)

            def sum_chosen(b):
                n = parity(b)
                dve.wait_ge(replaced_done, at(b, 1, 1))
                dve.wait_ge(exp_done, at(b, 1, 1))
                nc.vector.scalar_tensor_tensor(out=chosen[n][:, :], in0=replaced[n][:, 0:E], scalar=BORDER,
                                               in1=expo[n][:, :], op0=ALU.is_lt, op1=ALU.mult,
                                               accum_out=chosen_sum[n][:, 0:1]).then_inc(chosen_done, 1)
                dve.wait_ge(chosen_done, at(b, 1, 1))
                nc.vector.tensor_scalar(coeff_den[n][:, :], exp_sum[n][:, :], FFN_EPS, chosen_sum[n][:, 0:1],
                                        ALU.mult, ALU.add).then_inc(coeff_den_done, 1)
                dve.wait_ge(coeff_den_done, at(b, 1, 1))
                nc.vector.reciprocal(coeff_rec[n][:, :], coeff_den[n][:, :]).then_inc(coeff_rec_done, 1)

            def weigh(b):
                n = parity(b)
                dve.wait_ge(coeff_ps, at(b, 1, 1))
                dve.wait_ge(coeff_rec_done, at(b, 1, 1))
                nc.vector.tensor_scalar(coeff[n][:, :], ps_a[:, E + S:E + S + K], coeff_rec[n][:, 0:1], None,
                                        ALU.mult).then_inc(coeff_done, 1)

            def gate(b, half):
                dve.wait_ge(tanh_done, at(b, 2, half + 1))
                nc.vector.scalar_tensor_tensor(out=gated[half][:, :], in0=tanh_g[half][:, :], scalar=1.0,
                                               in1=gate_bank(b, half)[:, :], op0=ALU.add,
                                               op1=ALU.mult).then_inc(gated_done, 1)

            def basis(b, half, part):
                n = parity(b)
                dve.wait_ge(gated_done, at(b, 2, half + 1))
                dve.wait_ge(up_ps, at(b, 2, half + 1))
                dve.wait_ge(coeff_done, at(b, 1, 1))
                wait(dve, z_done, b, 1, -1)
                for k in range(2 * part, 2 * part + 2):
                    t = nc.vector.scalar_tensor_tensor(
                        out=bases[n][:, half * HALF_K + k, :], in0=up_bank(b, half)[:, k * I:(k + 1) * I],
                        scalar=coeff[n][:, half * HALF_K + k:half * HALF_K + k + 1],
                        in1=gated[half][:, k * I:(k + 1) * I], op0=ALU.mult, op1=ALU.mult)
                if part == 1:
                    t.then_inc(bases_done, 1)

            def sum_bases(b):
                n = parity(b)
                dve.wait_ge(bases_done, at(b, 2, 2))
                dve.wait_ge(z_done, b)
                nc.vector.tensor_tensor(sum4[:, :, :], bases[n][:, 0:4, :], bases[n][:, 4:8, :],
                                        ALU.add).then_inc(sum_step, 1)
                dve.wait_ge(sum_step, at(b, 2, 1))
                nc.vector.tensor_tensor(sum2[:, :, :], sum4[:, 0:2, :], sum4[:, 2:4, :],
                                        ALU.add).then_inc(sum_step, 1)
                dve.wait_ge(sum_step, at(b, 2, 2))
                nc.vector.tensor_tensor(zsum[n][:, :], sum2[:, 0, :], sum2[:, 1, :],
                                        ALU.add).then_inc(z_done, 1)

            def gate_shared(b):
                dve.wait_ge(tanh_s_done, at(b, 1, 1))
                nc.vector.scalar_tensor_tensor(out=gated_s[:, :], in0=tanh_s[:, :], scalar=1.0,
                                               in1=shared_bank(b)[:, 0:SI], op0=ALU.add,
                                               op1=ALU.mult).then_inc(gated_s_done, 1)

            def shared_basis(b):
                n = parity(b)
                dve.wait_ge(gated_s_done, at(b, 1, 1))
                nc.vector.tensor_tensor(shared[n][:, :], shared_bank(b)[:, SI:2 * SI], gated_s[:, :],
                                        ALU.mult).then_inc(shared_done, 1)

            def hT(b):
                n = parity(b)
                dve.wait_ge(hT_hi_done, at(b, 1, 1))
                nc.vector.scalar_tensor_tensor(out=hT_lo[n][:, :, :].rearrange("p c s -> p (c s)"),
                                               in0=ps_b[:, 0:3 * S], scalar=0.5,
                                               in1=f32(hT_hi[n][:, :, :]).rearrange("p c s -> p (c s)"),
                                               op0=ALU.mult, op1=ALU.subtract).then_inc(hT_lo_done, 1)

            def output(b):
                n = parity(b)
                dve.wait_ge(out_ps, at(b, 1, 1))
                if isinstance(b, tuple) or b >= 2:
                    dve.wait_ge(out_stored[n], by_parity(shift(b, -2)))
                nc.vector.tensor_tensor(out_sb[n][:, :], ps_b[:, 0:D], row(rows, b),
                                        ALU.add).then_inc(out_done, 1)

            def step(b, n):
                e, f, g = shift(b, -1), shift(b, -2), shift(b, -3)
                now, router, ffn, end = has(n, 0), has(n, -1), has(n, -2), has(n, -3)
                ahead, ahead2 = has(n, 1), has(n, 2)
                f_last = ffn and is_last(f)
                if router:
                    residual(e)
                if router:
                    moments2_of(e)
                if n == 1:
                    weight_lo(4)
                if ahead2 and n != 0:
                    moments_of(shift(b, 2))
                if router:
                    normalize2(e)
                if ahead2:
                    normalize(shift(b, 2))
                if ahead:
                    maxima(shift(b, 1), 0)
                if f_last:
                    gate_shared(f)
                    shared_basis(f)
                if ffn:
                    gate(f, 0)
                if router:
                    yT(e)
                if ahead2:
                    q_lo(shift(b, 2))
                if f_last and f == B - 1:
                    weigh(f)
                if ffn:
                    basis(f, 0, 0)
                if ahead:
                    maxima(shift(b, 1), 1)
                if ffn:
                    basis(f, 0, 1)
                if end:
                    hT(g)
                if n == 2:
                    weight_lo(5)
                    weight_lo(6)
                if ahead:
                    maxima(shift(b, 1), 2)
                if router:
                    choose(e)
                if ffn:
                    gate(f, 1)
                if router:
                    sum_chosen(e)
                if ahead:
                    maxima(shift(b, 1), 3)
                    split_max(shift(b, 1))
                if ffn:
                    basis(f, 1, 0)
                if now:
                    divide(b)
                if router and not f_last:
                    weigh(e)
                if ffn:
                    basis(f, 1, 1)
                if ffn and not f_last:
                    gate_shared(f)
                if now:
                    attnT(b)
                if ffn and not f_last:
                    shared_basis(f)
                if f_last and f == B - 1:
                    sum_bases(f)
                if end:
                    output(g)
                if n == 0:
                    weight_lo(3)

            run(dve, step)


_INS = ['x', 'ctx_512', 'L0_xattn_Wc', 'L0_xattn_bc', 'L0_ffn_w_router', 'L0_ffn_w_gate', 'L0_ffn_w_up',
        'L0_ffn_w_down', 'L0_ffn_amplitudes', 'L0_ffn_expert_scale', 'L0_ffn_shared_w_gate',
        'L0_ffn_shared_w_up', 'L0_ffn_shared_w_down']
_OUT = ((16, 128, 256), 'float32')


def kernel(**inputs):
    import numpy as _np
    import concourse.bacc as _bacc
    from concourse import mybir as _mybir
    from concourse.bass_utils import run_bass_kernel_spmd as _run

    nc = _bacc.Bacc("TRN2", target_bir_lowering=False, num_devices=1)
    arrays, args = {}, []
    for name in _INS:
        a = _np.ascontiguousarray(inputs[name])
        arrays[f"in_{name}_dram"] = a
        args.append(nc.dram_tensor(f"in_{name}_dram", a.shape, _mybir.dt.from_np(a.dtype), kind="ExternalInput").ap())
    args.append(nc.dram_tensor("out_0_dram", _OUT[0], _mybir.dt.from_np(_np.dtype(_OUT[1])),
                               kind="ExternalOutput").ap())
    build(nc, *args)
    r = _run(nc, [arrays], core_ids=[0])
    return r.results[0]["out_0_dram"]
```
